# Optimizing a Trainium2 kernel written in Bass

```python
import numpy as np
import jax
import jax.numpy as jnp

def _softmax(x, axis=-1):
    return jax.nn.softmax(x, axis=axis)

def _gelu(x):
    return jax.nn.gelu(x, approximate=True)

def _silu(x):
    return jax.nn.silu(x)

def _sigmoid(x):
    return jax.nn.sigmoid(x)

def _layernorm(x, axis=-1, eps=1e-05):
    m = jnp.mean(x, axis=axis, keepdims=True)
    v = jnp.var(x, axis=axis, keepdims=True)
    return (x - m) / jnp.sqrt(v + eps)

def _scatter_add(tgt, idx, src, axis=0):
    return tgt.at[idx].add(src)

def _segment_sum(src, seg, n):
    return jax.ops.segment_sum(src, seg, n)
kernel_name = 'mk_seq_preln_d2_jaxref_r8_cf7c97'

def setup_inputs(seed: int=0):
    np.random.seed(seed)
    _w = jnp.asarray

    def _L0_attn_setup():
        import jax, jax.numpy as jnp
        import numpy as np
        from jax import lax
        H = 64
        P = 64
        N = 128
        G = 8
        K = 4
        D_MODEL = 512
        I = H * P
        GN = G * N
        CONV_DIM = I + 2 * GN
        PROJ = I + CONV_DIM + H
        EPS = 1e-05
        GROUP_SIZE = I // G

        def _reference_tuple_inner(hidden_states, in_proj_w, conv_weight, conv_bias, dt_bias, A_log, D, norm_weight, out_proj_w):
            B, L, _ = hidden_states.shape
            proj = jnp.einsum('bld,pd->blp', hidden_states, in_proj_w)
            gate = proj[..., :I]
            hbc = proj[..., I:I + CONV_DIM]
            dt = proj[..., -H:]
            pad = jnp.pad(hbc, ((0, 0), (K - 1, 0), (0, 0)))
            conv = conv_bias
            for k in range(K):
                conv = conv + pad[:, k:k + L, :] * conv_weight[:, k]
            xBC = jax.nn.silu(conv)
            x = xBC[..., :I].reshape(B, L, H, P)
            Bm = xBC[..., I:I + GN].reshape(B, L, G, N)
            Cm = xBC[..., I + GN:].reshape(B, L, G, N)
            hpg = H // G
            B_h = jnp.repeat(Bm, hpg, axis=2)
            C_h = jnp.repeat(Cm, hpg, axis=2)
            dt_p = jax.nn.softplus(dt + dt_bias)
            A = -jnp.exp(A_log)
            dA = jnp.exp(dt_p * A)
            dtx = dt_p[..., None] * x

            def step(state, inp):
                dA_t, dtx_t, B_t, C_t = inp
                state = state * dA_t[..., None, None] + dtx_t[..., None] * B_t[:, :, None, :]
                y_t = jnp.einsum('bhpn,bhn->bhp', state, C_t)
                return (state, y_t)
            xs = (jnp.moveaxis(dA, 1, 0), jnp.moveaxis(dtx, 1, 0), jnp.moveaxis(B_h, 1, 0), jnp.moveaxis(C_h, 1, 0))
            state0 = jnp.zeros((B, H, P, N), jnp.float32)
            final_state, ys = lax.scan(step, state0, xs)
            y = jnp.moveaxis(ys, 0, 1) + x * D[None, None, :, None]
            y = y.reshape(B, L, I)
            yg = y.reshape(B, L, G, GROUP_SIZE)
            var = jnp.mean(yg * yg, axis=-1, keepdims=True)
            yn = (yg * lax.rsqrt(var + EPS)).reshape(B, L, I) * norm_weight
            yn = yn * jax.nn.silu(gate)
            out = jnp.einsum('bli,di->bld', yn, out_proj_w)
            conv_state_new = jnp.moveaxis(hbc[:, L - (K - 1):, :], 1, 2)
            return (out, conv_state_new, final_state)
        key = jax.random.key(seed)
        ks = jax.random.split(key, 6)
        B, L = (2, 256)
        s = 0.02
        return {'hidden_states': jax.random.normal(ks[0], (B, L, D_MODEL), jnp.float32), 'in_proj_w': jax.random.normal(ks[1], (PROJ, D_MODEL), jnp.float32) * s, 'conv_weight': jax.random.normal(ks[2], (CONV_DIM, K), jnp.float32) * s, 'conv_bias': jnp.zeros((CONV_DIM,), jnp.float32), 'dt_bias': jnp.ones((H,), jnp.float32), 'A_log': jnp.log(jnp.arange(1, H + 1, dtype=jnp.float32)), 'D': jnp.ones((H,), jnp.float32), 'norm_weight': jnp.ones((I,), jnp.float32), 'out_proj_w': jax.random.normal(ks[3], (D_MODEL, I), jnp.float32) * s}
    _L0_attn_in = _L0_attn_setup()

    def _L0_ffn_setup():
        import jax, jax.numpy as jnp
        import numpy as np
        HID = 512
        INTER = 1376
        BITS = 4
        PACK = 8
        MAXQ = 15
        GROUP = 128

        def _dequant(qweight, scales, qzeros, g_idx):
            shifts = jnp.arange(PACK, dtype=jnp.uint32) * BITS
            qw = qweight.astype(jnp.uint32)
            w = (qw[:, None, :] >> shifts[None, :, None] & MAXQ).reshape(-1, qweight.shape[1])
            qz = qzeros.astype(jnp.uint32)
            z = ((qz[:, :, None] >> shifts[None, None, :] & MAXQ) + 1).reshape(qzeros.shape[0], -1)
            s = scales[g_idx]
            return (w.astype(scales.dtype) - z[g_idx].astype(scales.dtype)) * s
        key = jax.random.key(seed)
        ks = jax.random.split(key, 16)

        def qw(k, K, N):
            return jax.random.randint(k, (K // PACK, N), 0, 2147483647, dtype=jnp.int32)

        def qz(k, G, N):
            return jax.random.randint(k, (G, N // PACK), 0, 2147483647, dtype=jnp.int32)

        def sc(k, G, N):
            return jax.random.uniform(k, (G, N), jnp.float32, 0.001, 0.01)
        Gk = HID // GROUP
        Gd = INTER // GROUP
        return {'x': jax.random.normal(ks[0], (4, 256, HID), jnp.float32), 'gate_qweight': qw(ks[1], HID, INTER), 'gate_scales': sc(ks[2], Gk, INTER), 'gate_qzeros': qz(ks[3], Gk, INTER), 'gate_g_idx': (jnp.arange(HID) // GROUP).astype(jnp.int32), 'up_qweight': qw(ks[4], HID, INTER), 'up_scales': sc(ks[5], Gk, INTER), 'up_qzeros': qz(ks[6], Gk, INTER), 'up_g_idx': (jnp.arange(HID) // GROUP).astype(jnp.int32), 'down_qweight': qw(ks[7], INTER, HID), 'down_scales': sc(ks[8], Gd, HID), 'down_qzeros': qz(ks[9], Gd, HID), 'down_g_idx': (jnp.arange(INTER) // GROUP).astype(jnp.int32)}
    _L0_ffn_in = _L0_ffn_setup()

    def _L1_attn_setup():
        import jax, jax.numpy as jnp
        import numpy as np
        EMB = 512
        HEADS = 32
        SCALE = 4
        D = EMB // HEADS
        HKV = HEADS // SCALE
        B, S = (2, 256)
        key = jax.random.key(seed)
        ks = jax.random.split(key, 7)
        std = 0.02
        return {'x': jax.random.normal(ks[0], (B, S, EMB), jnp.float32), 'Wq': jax.random.normal(ks[1], (EMB, D, HEADS), jnp.float32) * std, 'bq': jnp.zeros((D, HEADS), jnp.float32), 'Wk': jax.random.normal(ks[2], (EMB, D, HKV), jnp.float32) * std, 'bk': jnp.zeros((D, HKV), jnp.float32), 'Wv': jax.random.normal(ks[3], (EMB, D, HKV), jnp.float32) * std, 'bv': jnp.zeros((D, HKV), jnp.float32)}
    _L1_attn_in = _L1_attn_setup()

    def _L1_ffn_setup():
        import jax, jax.numpy as jnp
        import numpy as np
        NUM_EXPERTS = 8
        TOP_K = 2
        RANK = 16
        LORA_ALPHA = 32
        SCALING = LORA_ALPHA / RANK
        key = jax.random.key(seed)
        ks = jax.random.split(key, 6)
        B, S, D_IN, D_OUT = (4, 256, 512, 512)
        x = jax.random.normal(ks[0], (B, S, D_IN), dtype=jnp.float32)
        W_base = jax.random.normal(ks[1], (D_OUT, D_IN), dtype=jnp.float32) * 0.02
        b_base = jax.random.normal(ks[2], (D_OUT,), dtype=jnp.float32) * 0.02
        W_router = jax.random.normal(ks[3], (NUM_EXPERTS, D_IN), dtype=jnp.float32) * 0.02
        A = jax.random.normal(ks[4], (NUM_EXPERTS, RANK, D_IN), dtype=jnp.float32) * 0.02
        Bm = jax.random.normal(ks[5], (D_OUT, RANK), dtype=jnp.float32) * 0.02
        Bm = jnp.broadcast_to(Bm, (NUM_EXPERTS, D_OUT, RANK)) * jnp.arange(1, NUM_EXPERTS + 1, dtype=jnp.float32)[:, None, None] * 0.2
        return {'x': x, 'W_base': W_base, 'b_base': b_base, 'W_router': W_router, 'A': A, 'B': Bm}
    _L1_ffn_in = _L1_ffn_setup()
    _d = {'L0_attn_hidden_states': _L0_attn_in['hidden_states'], 'L0_attn_in_proj_w': _L0_attn_in['in_proj_w'], 'L0_attn_conv_weight': _L0_attn_in['conv_weight'], 'L0_attn_conv_bias': _L0_attn_in['conv_bias'], 'L0_attn_dt_bias': _L0_attn_in['dt_bias'], 'L0_attn_A_log': _L0_attn_in['A_log'], 'L0_attn_D': _L0_attn_in['D'], 'L0_attn_norm_weight': _L0_attn_in['norm_weight'], 'L0_attn_out_proj_w': _L0_attn_in['out_proj_w'], 'L0_ffn_gate_qweight': _L0_ffn_in['gate_qweight'], 'L0_ffn_gate_scales': _L0_ffn_in['gate_scales'], 'L0_ffn_gate_qzeros': _L0_ffn_in['gate_qzeros'], 'L0_ffn_gate_g_idx': _L0_ffn_in['gate_g_idx'], 'L0_ffn_up_qweight': _L0_ffn_in['up_qweight'], 'L0_ffn_up_scales': _L0_ffn_in['up_scales'], 'L0_ffn_up_qzeros': _L0_ffn_in['up_qzeros'], 'L0_ffn_up_g_idx': _L0_ffn_in['up_g_idx'], 'L0_ffn_down_qweight': _L0_ffn_in['down_qweight'], 'L0_ffn_down_scales': _L0_ffn_in['down_scales'], 'L0_ffn_down_qzeros': _L0_ffn_in['down_qzeros'], 'L0_ffn_down_g_idx': _L0_ffn_in['down_g_idx'], 'L1_attn_Wq': _L1_attn_in['Wq'], 'L1_attn_bq': _L1_attn_in['bq'], 'L1_attn_Wk': _L1_attn_in['Wk'], 'L1_attn_bk': _L1_attn_in['bk'], 'L1_attn_Wv': _L1_attn_in['Wv'], 'L1_attn_bv': _L1_attn_in['bv'], 'L1_ffn_W_base': _L1_ffn_in['W_base'], 'L1_ffn_b_base': _L1_ffn_in['b_base'], 'L1_ffn_W_router': _L1_ffn_in['W_router'], 'L1_ffn_A': _L1_ffn_in['A'], 'L1_ffn_B': _L1_ffn_in['B']}
    _x0 = _d['L0_attn_hidden_states']
    _d['L0_attn_hidden_states'] = jax.random.normal(jax.random.fold_in(jax.random.key(seed), 1), (1, 1024, 512), dtype=_x0.dtype)
    del _x0
    return _d

def reference(L0_attn_hidden_states, L0_attn_in_proj_w, L0_attn_conv_weight, L0_attn_conv_bias, L0_attn_dt_bias, L0_attn_A_log, L0_attn_D, L0_attn_norm_weight, L0_attn_out_proj_w, L0_ffn_gate_qweight, L0_ffn_gate_scales, L0_ffn_gate_qzeros, L0_ffn_gate_g_idx, L0_ffn_up_qweight, L0_ffn_up_scales, L0_ffn_up_qzeros, L0_ffn_up_g_idx, L0_ffn_down_qweight, L0_ffn_down_scales, L0_ffn_down_qzeros, L0_ffn_down_g_idx, L1_attn_Wq, L1_attn_bq, L1_attn_Wk, L1_attn_bk, L1_attn_Wv, L1_attn_bv, L1_ffn_W_base, L1_ffn_b_base, L1_ffn_W_router, L1_ffn_A, L1_ffn_B):

    def _L0_attn_ref(hidden_states, in_proj_w, conv_weight, conv_bias, dt_bias, A_log, D, norm_weight, out_proj_w):
        import jax, jax.numpy as jnp
        import numpy as np
        from jax import lax
        H = 64
        P = 64
        N = 128
        G = 8
        K = 4
        D_MODEL = 512
        I = H * P
        GN = G * N
        CONV_DIM = I + 2 * GN
        PROJ = I + CONV_DIM + H
        EPS = 1e-05
        GROUP_SIZE = I // G

        def _reference_tuple_inner(hidden_states, in_proj_w, conv_weight, conv_bias, dt_bias, A_log, D, norm_weight, out_proj_w):
            B, L, _ = hidden_states.shape
            proj = jnp.einsum('bld,pd->blp', hidden_states, in_proj_w)
            gate = proj[..., :I]
            hbc = proj[..., I:I + CONV_DIM]
            dt = proj[..., -H:]
            pad = jnp.pad(hbc, ((0, 0), (K - 1, 0), (0, 0)))
            conv = conv_bias
            for k in range(K):
                conv = conv + pad[:, k:k + L, :] * conv_weight[:, k]
            xBC = jax.nn.silu(conv)
            x = xBC[..., :I].reshape(B, L, H, P)
            Bm = xBC[..., I:I + GN].reshape(B, L, G, N)
            Cm = xBC[..., I + GN:].reshape(B, L, G, N)
            hpg = H // G
            B_h = jnp.repeat(Bm, hpg, axis=2)
            C_h = jnp.repeat(Cm, hpg, axis=2)
            dt_p = jax.nn.softplus(dt + dt_bias)
            A = -jnp.exp(A_log)
            dA = jnp.exp(dt_p * A)
            dtx = dt_p[..., None] * x

            def step(state, inp):
                dA_t, dtx_t, B_t, C_t = inp
                state = state * dA_t[..., None, None] + dtx_t[..., None] * B_t[:, :, None, :]
                y_t = jnp.einsum('bhpn,bhn->bhp', state, C_t)
                return (state, y_t)
            xs = (jnp.moveaxis(dA, 1, 0), jnp.moveaxis(dtx, 1, 0), jnp.moveaxis(B_h, 1, 0), jnp.moveaxis(C_h, 1, 0))
            state0 = jnp.zeros((B, H, P, N), jnp.float32)
            final_state, ys = lax.scan(step, state0, xs)
            y = jnp.moveaxis(ys, 0, 1) + x * D[None, None, :, None]
            y = y.reshape(B, L, I)
            yg = y.reshape(B, L, G, GROUP_SIZE)
            var = jnp.mean(yg * yg, axis=-1, keepdims=True)
            yn = (yg * lax.rsqrt(var + EPS)).reshape(B, L, I) * norm_weight
            yn = yn * jax.nn.silu(gate)
            out = jnp.einsum('bli,di->bld', yn, out_proj_w)
            conv_state_new = jnp.moveaxis(hbc[:, L - (K - 1):, :], 1, 2)
            return (out, conv_state_new, final_state)
        return _reference_tuple_inner(hidden_states, in_proj_w, conv_weight, conv_bias, dt_bias, A_log, D, norm_weight, out_proj_w)[0]

    def _L0_ffn_ref(x, gate_qweight, gate_scales, gate_qzeros, gate_g_idx, up_qweight, up_scales, up_qzeros, up_g_idx, down_qweight, down_scales, down_qzeros, down_g_idx):
        import jax, jax.numpy as jnp
        import numpy as np
        HID = 512
        INTER = 1376
        BITS = 4
        PACK = 8
        MAXQ = 15
        GROUP = 128

        def _dequant(qweight, scales, qzeros, g_idx):
            shifts = jnp.arange(PACK, dtype=jnp.uint32) * BITS
            qw = qweight.astype(jnp.uint32)
            w = (qw[:, None, :] >> shifts[None, :, None] & MAXQ).reshape(-1, qweight.shape[1])
            qz = qzeros.astype(jnp.uint32)
            z = ((qz[:, :, None] >> shifts[None, None, :] & MAXQ) + 1).reshape(qzeros.shape[0], -1)
            s = scales[g_idx]
            return (w.astype(scales.dtype) - z[g_idx].astype(scales.dtype)) * s
        Wg = _dequant(gate_qweight, gate_scales, gate_qzeros, gate_g_idx)
        Wu = _dequant(up_qweight, up_scales, up_qzeros, up_g_idx)
        Wd = _dequant(down_qweight, down_scales, down_qzeros, down_g_idx)
        xf = x.reshape(-1, x.shape[-1])
        h = jax.nn.silu(xf @ Wg) * (xf @ Wu)
        out = h @ Wd
        return out.reshape(x.shape[:-1] + (Wd.shape[1],))

    def _L1_attn_ref(x, Wq, bq, Wk, bk, Wv, bv):
        import jax, jax.numpy as jnp
        import numpy as np
        EMB = 512
        HEADS = 32
        SCALE = 4
        D = EMB // HEADS
        HKV = HEADS // SCALE
        B, S = (2, 256)
        q = jnp.einsum('bse,edh->bsdh', x, Wq) + bq
        k = jnp.einsum('bse,edh->bsdh', x, Wk) + bk
        v = jnp.einsum('bse,edh->bsdh', x, Wv) + bv
        k = jnp.repeat(k, SCALE, axis=-1)
        v = jnp.repeat(v, SCALE, axis=-1)
        scores = jnp.einsum('bsdh,bseh->bsde', q, k) / np.float32(np.sqrt(D))
        attn = jax.nn.softmax(scores, axis=-1)
        out = jnp.einsum('bsde,bseh->bsdh', attn, v)
        return out.reshape(x.shape[:-1] + (EMB,))

    def _L1_ffn_ref(x, W_base, b_base, W_router, A, B):
        import jax, jax.numpy as jnp
        import numpy as np
        NUM_EXPERTS = 8
        TOP_K = 2
        RANK = 16
        LORA_ALPHA = 32
        SCALING = LORA_ALPHA / RANK
        bs, seq, d_in = x.shape
        T = bs * seq
        xf = x.reshape(T, d_in)
        base = xf @ W_base.T + b_base
        logits = xf @ W_router.T
        rw, sel = jax.lax.top_k(logits, TOP_K)
        rw = jax.nn.softmax(rw, axis=-1)
        onehot = jax.nn.one_hot(sel, NUM_EXPERTS, dtype=rw.dtype)
        w = jnp.einsum('tk,tke->te', rw, onehot)
        h = jnp.einsum('td,erd->ter', xf, A)
        lora = jnp.einsum('ter,te,eor->to', h, w, B) * SCALING
        return (base + lora).reshape(bs, seq, -1)
    x = L0_attn_hidden_states
    x = x + _L0_attn_ref(_layernorm(x, axis=-1), L0_attn_in_proj_w, L0_attn_conv_weight, L0_attn_conv_bias, L0_attn_dt_bias, L0_attn_A_log, L0_attn_D, L0_attn_norm_weight, L0_attn_out_proj_w)
    x = x + _L0_ffn_ref(_layernorm(x, axis=-1), L0_ffn_gate_qweight, L0_ffn_gate_scales, L0_ffn_gate_qzeros, L0_ffn_gate_g_idx, L0_ffn_up_qweight, L0_ffn_up_scales, L0_ffn_up_qzeros, L0_ffn_up_g_idx, L0_ffn_down_qweight, L0_ffn_down_scales, L0_ffn_down_qzeros, L0_ffn_down_g_idx)
    x = x + _L1_attn_ref(_layernorm(x, axis=-1), L1_attn_Wq, L1_attn_bq, L1_attn_Wk, L1_attn_bk, L1_attn_Wv, L1_attn_bv)
    x = x + _L1_ffn_ref(_layernorm(x, axis=-1), L1_ffn_W_base, L1_ffn_b_base, L1_ffn_W_router, L1_ffn_A, L1_ffn_B)
    return x

_drawn_inputs = setup_inputs


def setup_inputs(seed=0):
    import zlib

    import numpy as np

    out = dict(_drawn_inputs(seed))
    spreads = {'L0_attn_conv_bias': (0.0, 0.1),
     'L0_attn_dt_bias': (1.0, 0.6),
     'L0_attn_D': (1.0, 0.2),
     'L0_attn_norm_weight': (1.0, 0.2),
     'L1_attn_bq': (0.0, 0.8),
     'L1_attn_bk': (0.0, 0.8),
     'L1_attn_bv': (0.0, 0.27)}
    factors = {'L0_attn_A_log': 8.0, 'L1_ffn_b_base': 4.098}
    for name, (base, spread) in spreads.items():
        noise = np.random.default_rng([zlib.crc32(name.encode()), seed]).standard_normal(out[name].shape)
        drawn = base * np.exp(spread * noise) if base else spread * noise
        out[name] = jnp.asarray(drawn.astype(out[name].dtype))
    for name, factor in factors.items():
        out[name] = (out[name] * factor).astype(out[name].dtype)
    return out
```

```python
from contextlib import ExitStack

import numpy as np

import concourse.bass as bass
from concourse import mybir

F32 = mybir.dt.float32
F32R = mybir.dt.float32r
BF16 = mybir.dt.bfloat16
I32 = mybir.dt.int32
U32 = mybir.dt.uint32
ALU = mybir.AluOpType
ACT = mybir.ActivationFunctionType
AX = mybir.AxisListType

P = 128
L = 1024
D = 512
KT = D // P
HALF = L // 2
NC = L // P
CH = NC // 2

H = 64
HD = 64
G = 8
HG = H // G
GW = HG * HD
NS = 128
TAPS = 4
TILES = GW // P + 2
TB, TC = TILES - 2, TILES - 1
WT = TILES + KT + GW // P
EPS = 1e-5
LOG_FLOOR = -87.0
PART = 3
NTHR = 63
KD = PART + PART * HG + NTHR
MASK = -32768.0


def wait(eng, sem, count):
    if isinstance(count, int) and count <= 0:
        return
    eng.wait_ge(sem, count)


def at(eng, value):
    return value if isinstance(value, int) else eng.snap(value)


def three_pass(pe, out, lhs, rhs, k_tiles):
    last = None
    for k in range(k_tiles):
        (lh, ll), (rh, rl) = lhs(k), rhs(k)
        for n, (a, b) in enumerate(((lh, rh), (lh, rl), (ll, rh))):
            last = pe.matmul(out, a, b, start=(k == 0 and n == 0), stop=(k == k_tiles - 1 and n == 2))
    return last


def mixer(nc, io, ctx, x_res, ident):
    def sb(name, shape, dt=F32):
        return ctx.enter_context(nc.sbuf_tensor(name, shape, dt))

    def pb(name):
        return ctx.enter_context(nc.psum_tensor(name, [P, 512], F32))

    def sem(name):
        return ctx.enter_context(nc.semaphore(name))

    xn_hi = sb("xn_hi", [P, KT, L], F32R)
    xn_lo = sb("xn_lo", [P, KT, L], F32R)
    w_raw = sb("w_raw", [P, 2, 512])
    w_hi = sb("w_hi", [P, WT, 512], F32R)
    w_lo = sb("w_lo", [P, WT, 512], F32R)
    conv_w = sb("conv_taps", [P, G, TILES, TAPS + 1])
    norm_w = sb("norm_scale", [P, G, GW // P])
    pre = sb("pre", [P, 2, HALF + TAPS - 1])
    halo = sb("halo", [P, TILES, TAPS - 1])
    conv = sb("conv", [P, 2, HALF])
    conv_th = sb("conv_th", [P, 2, HALF])
    xbc = sb("xbc", [P, TILES, L])
    d_lhs = sb("decay_lhs", [KD, 2, P], BF16)
    d_rhs = sb("decay_rhs", [KD, 2, HG * P], BF16)
    em = sb("em", [P, 2, HG * P])
    gm = sb("gm", [P, P])
    b_tok = sb("b_tok", [P, P])
    xs = sb("xs", [P, 2, GW])
    x_dt = sb("x_dt", [P, GW])
    x_w = sb("x_w", [P, GW])
    x_d = sb("x_d", [P, GW])
    y = sb("y", [P, 2, GW])
    gate_th = sb("gate_th", [P, GW])
    gate = sb("gate", [P, GW])
    z = sb("z", [P, GW])
    zt_hi = sb("zt_hi", [P, GW // P, P], F32R)
    zt_lo = sb("zt_lo", [P, GW // P, P], F32R)
    junk = sb("junk", [P, GW])
    state = sb("state", [P, GW])
    state_dec = sb("state_dec", [P, GW])
    dt_t = sb("dt_t", [P, NC, H])
    dtw_t = sb("dtw_t", [P, NC, H])
    ecum_t = sb("ecum_t", [P, NC, H])
    etot_t = sb("etot_t", [P, NC, H])
    head_g = sb("head_g", [P, 4, NC, HG])
    d_g = sb("d_g", [P, HG])
    tri = sb("tri_mask", [P, P])
    d_b = sb("d_b", [P, H])
    head_c = sb("head_consts", [P, 4])
    stats = sb("stats", [P, NC, 6])
    mean_var = sb("mean_var", [P, NC, 2])
    rstd = sb("rstd", [P, NC])
    m_half = sb("m_half", [P, 1])
    ss = sb("ss", [P, 2])
    ssv = sb("ssv", [P, 2])
    g_rstd = sb("g_rstd", [P, 2])
    xnt = xs

    p_tile, p_gate, p_d0, p_d1 = pb("p_tile"), pb("p_gate"), pb("p_d0"), pb("p_d1")
    p_x, p_in, p_y, p_gb = pb("p_x"), pb("p_in"), pb("p_y"), pb("p_gb")

    parts = nc.dram_tensor("cum_parts", [G, PART, HG, L], BF16, kind="Internal").ap()
    w_rows = io["w"].rearrange("n p c -> (n p) c")

    s_x = [sem(f"s_x{i}") for i in range(NC)]
    s_const = sem("s_const")
    s_halved = sem("s_halved")
    s_raw = [sem("s_raw0"), sem("s_raw1")]
    s_dl = [sem("s_dl0"), sem("s_dl1")]
    s_parts = sem("s_parts")
    s_dconst = sem("s_dconst")
    ln_st, ln_var, ln_rs, ln_xn, ln_tr, ln_hi, ln_lo = (sem(f"ln_{k}") for k in "abcdefg")
    dt_mm, dt_ve, dt_ac, dt_tp = (sem(f"dt_{k}") for k in ("mm", "ve", "ac", "tp"))
    s_xt, s_gb, s_d, s_prj, s_gate, s_zt, s_out, s_inter, s_intra, s_stn = (
        sem(f"pe_{k}") for k in ("xt", "gb", "d", "prj", "gate", "zt", "out", "inter", "intra", "stn"))
    s_xs, s_e, s_cin, s_th, s_tg, s_zhi, s_ss, s_whi = (
        sem(f"act_{k}") for k in ("xs", "e", "cin", "th", "tg", "zhi", "ss", "whi"))
    s_head = sem("ve_head")
    s_gm, s_m, s_halo, s_tap, s_xc, s_sg, s_zlo, s_res, s_t, s_y, s_z, s_stu, s_v, s_wloo = (
        sem(f"ve_{k}") for k in ("gm", "m", "halo", "tap", "xc", "sg", "zlo", "res", "t", "y", "z",
                                 "stu", "v", "wloo"))
    s_xdt, s_xw, s_xd, s_std, s_txd, s_rs, s_wlo = (
        sem(f"pool_{k}") for k in ("xdt", "xw", "xd", "std", "txd", "rs", "wlo"))

    MADE_IN = [(0, 1), (2, 3), (4,), (5,)]
    SPLIT_IN = {1: (0, 1), 2: (2, 3), 3: (4,), 4: (5,), 7: (6, 7, 8, 9)}
    LAST = NC * G - 1

    def half_cols(hf):
        return slice(hf * HALF, (hf + 1) * HALF)

    def conv_tiles(g, last, c):
        def made(c):
            if last and c >= CH:
                return []
            half = 2 * g + c // CH + 1
            return [(half * TILES + j, g + c // CH, j, 1 - c // CH) for j in MADE_IN[c % CH]]
        return (made(c - 1)[1:] if c % CH else []), made(c)

    def heads(k, c):
        return head_g[:, k, c, :].unsqueeze(2).broadcast_to([P, HG, HD])

    DT, DTW, ECUM, ETOT = range(4)

    def by_head(ap):
        return ap.rearrange("p (h d) -> p h d", h=HG)

    def rows(ap):
        return ap.rearrange("p (a t) -> p a t", a=2)
    t_v = xbc[0:H, 0:2, HALF:L]
    t_a = xbc[0:H, 2:4, HALF:L]
    t_dt = xbc[0:H, 4:6, HALF:L]
    t_e = rows(em[0:H, 0, :])
    t_cum = rows(em[0:H, 1, :])
    t_w = y[0:H, :, :]
    t_r = pre[0:H, :, 0:HALF]
    t_rem = conv[0:H, :, :]
    t_parts = [rows(x[0:H, 0:GW].bitcast(BF16)) for x in (x_dt, x_w, x_d)]
    t_mask = rows(junk[0:H, :].bitcast(BF16))

    block = ctx.enter_context(nc.Block())

    @block.sync
    def _(sp):
        for c in range(NC):
            sp.dma_start(x_res[:, c, :], io["x"][c * P:(c + 1) * P, :]).then_inc(s_x[c], 16)
            if c == 1:
                sp.dma_start(ident[:], io["ident"]).then_inc(s_const, 16)
                sp.dma_start(head_c[:, 0:2], io["head_c"]).then_inc(s_const, 16)
                sp.dma_start(z[:], io["w_dt"]).then_inc(s_const, 16)
        sp.dma_start(conv_w[:], io["conv_w"]).then_inc(s_const, 16)
        sp.dma_start(norm_w[:], io["norm_w"]).then_inc(s_const, 16)
        sp.dma_start(tri[:], io["tri"]).then_inc(s_const, 16)
        sp.dma_start(d_b[:], io["d"].broadcast_to([P, H])).then_inc(s_const, 16)
        for i in range(2):
            sp.dma_start(d_lhs[:, i, :], io["d_lhs"]).then_inc(s_dconst, 16)
            sp.dma_start(d_rhs[:, i, :], io["d_rhs"]).then_inc(s_dconst, 16)

        def load_w(g, w):
            row = at(sp, (g * WT + w) * P)
            if w < 2:
                split, count = s_wloo, g * (GW // P) - 1 + w
            elif w < TILES + KT + 2:
                split, count = s_wlo, g * (TILES + KT) + w - 1
            else:
                split, count = s_wloo, g * (GW // P) + w - TILES - KT - 1
            wait(sp, split, at(sp, count))
            sp.dma_start(w_raw[:, w % 2, :], w_rows[bass.ds(row, P), :]).then_inc(s_raw[w % 2], 16)

        def load_d(g, c):
            n = g * NC + c
            lhs_row, rhs_row = at(sp, g * PART * HG), at(sp, g * PART)
            wait(sp, s_d, n - 1)
            cs = slice(c * P, (c + 1) * P)
            sp.dma_start(d_lhs[PART:PART + PART * HG, c % 2, :],
                         parts.rearrange("g k h t -> (g k h) t")[bass.ds(lhs_row, PART * HG), cs])\
                .then_inc(s_dl[c % 2], 16)
            sp.dma_start(d_rhs[0:PART, c % 2, :].rearrange("k (h t) -> k h t", h=HG),
                         parts.rearrange("g k h t -> (g k) h t")[bass.ds(rhs_row, PART), :, cs])\
                .then_inc(s_dl[c % 2], 16)

        for w in range(TILES + KT):
            load_w(0, w)
        wait(sp, dt_ve, 15)
        for k in range(PART):
            for g in range(G):
                sp.dma_start(parts[g, k].rearrange("h (a t) -> h a t", a=2), t_parts[k][g * HG:(g + 1) * HG])\
                    .then_inc(s_parts, 16)
        sp.wait_ge(s_parts, 16 * PART * G)
        sp.wait_ge(s_dconst, 64)
        load_d(0, 0)
        load_d(0, 1)

        def group(g, last):
            for c in range(NC):
                if c + 2 < NC:
                    load_d(g, c + 2)
                elif not last:
                    load_d(g + 1, c + 2 - NC)
                if not last:
                    for w in {0: (0, 1), 1: (2, 3), 2: (4, 5), 3: (6, 7), 7: (8, 9)}.get(c, ()):
                        load_w(g + 1, w)

        def out_weights(g):
            for w in range(TILES + KT, WT):
                load_w(g, w)

        out_weights(0)
        group(0, False)
        with sp.Fori(1, G - 1) as g:
            out_weights(g)
            group(g, False)
        out_weights(G - 1)
        group(G - 1, True)

    @block.gpsimd
    def _(pool):
        def group(g, last):
            for c in range(NC):
                n = g * NC + c
                st = g * (NC - 1) + c
                if c > 0:
                    pool.wait_ge(s_stu, n)
                    pool.tensor_tensor(by_head(state_dec[:]), by_head(state[:]), heads(ETOT, c), ALU.mult)\
                        .then_inc(s_std, 1)
                if c == 0:
                    pool.wait_ge(s_head, 5 * (g + 1))
                pool.wait_ge(s_xs, n + 1)
                wait(pool, s_stn, n)
                pool.tensor_tensor(by_head(x_w[:]), by_head(xs[:, c % 2, :]), heads(DTW, c), ALU.mult)\
                    .then_inc(s_xw, 1)
                wait(pool, s_intra, n)
                pool.tensor_tensor(by_head(x_dt[:]), by_head(xs[:, c % 2, :]), heads(DT, c), ALU.mult)\
                    .then_inc(s_xdt, 1)
                if not (isinstance(g, int) and n == 0):
                    norm(n - 1, (c - 1) % 2)
                wait(pool, s_y, n)
                pool.tensor_tensor(by_head(x_d[:]), by_head(xs[:, c % 2, :]),
                                   d_g[:].unsqueeze(2).broadcast_to([P, HG, HD]), ALU.mult)\
                    .then_inc(s_xd, 1)
                splits = () if last else SPLIT_IN.get(c, ())
                for w in splits[:2]:
                    w_rest(g + 1, w)
                if c > 0:
                    pool.wait_ge(s_t, st)
                    pool.wait_ge(s_xd, n + 1)
                    pool.tensor_tensor(y[:, c % 2, :], y[:, c % 2, :], x_d[:], ALU.add).then_inc(s_txd, 1)
                for w in splits[2:]:
                    w_rest(g + 1, w)

        def norm(m, slot):
            pool.wait_ge(s_v, m + 1)
            pool.tensor_tensor(g_rstd[:, slot:slot + 1], ssv[:, slot:slot + 1], m_half[:], ALU.pow).then_inc(s_rs, 1)

        def w_rest(g, w):
            n = g * WT + w
            pool.wait_ge(s_whi, n + 1)
            pool.tensor_tensor(w_lo[:, w, :], w_raw[:, w % 2, :], w_hi[:, w, :].bitcast(F32), ALU.subtract)\
                .then_inc(s_wlo, 1)

        pool.memset(m_half[:], -0.5).then_inc(ln_rs, 1)
        for w in range(2):
            w_rest(0, w)
        pool.wait_ge(ln_var, NC + 1)
        pool.wait_ge(ln_rs, 1)
        pool.tensor_tensor(rstd[:], rstd[:], m_half[:].broadcast_to([P, NC]), ALU.pow).then_inc(ln_rs, 1)
        for w in range(2, TILES + KT):
            w_rest(0, w)
        pool.wait_ge(s_parts, 16 * PART * G)
        group(0, False)
        with pool.Fori(1, G - 1) as g:
            group(g, False)
        group(G - 1, True)
        norm(LAST, (NC - 1) % 2)

    @block.scalar
    def _(act):
        def w_round(g, w):
            n = g * WT + w
            act.wait_ge(s_raw[w % 2], 16 * (g * (WT // 2) + w // 2 + 1))
            if w < TILES + KT:
                act.activation(w_hi[:, w, :], w_raw[:, w % 2, :], ACT.Copy).then_inc(s_whi, 1)
            else:
                k = w - TILES - KT
                act.activation(w_hi[:, w, :], w_raw[:, w % 2, :], ACT.Copy, scale=norm_w[:, bass.ds(g, 1), k])\
                    .then_inc(s_whi, 1)

        def tile_in(T, g, j):
            s = j % 2
            act.wait_ge(s_prj, T + 1)
            wait(act, s_xc, T - 1)
            act.activation(pre[:, s, TAPS - 1:], p_tile[:], ACT.Copy).then_inc(s_cin, 1)
            act.activation(conv[:, s, :], p_tile[:], ACT.Identity, bias=conv_w[:, bass.ds(g, 1), j, TAPS],
                           scale=conv_w[:, bass.ds(g, 1), j, TAPS - 1]).then_inc(s_cin, 1)

        def tile_tanh(T, j):
            act.wait_ge(s_tap, TAPS * (T + 1))
            act.activation(conv_th[:, j % 2, :], conv[:, j % 2, :], ACT.Tanh).then_inc(s_th, 1)

        def z_round(m):
            act.wait_ge(s_zt, m + 1)
            act.activation(zt_hi[:].rearrange("p k t -> p (k t)"), p_in[:], ACT.Copy).then_inc(s_zhi, 1)

        def gate_tanh(m):
            act.wait_ge(s_gate, m + 1)
            wait(act, s_sg, m)
            act.activation(gate_th[:], p_gate[:], ACT.Tanh, scale=0.5).then_inc(s_tg, 1)

        def group(g, last):
            for c in range(NC):
                n = g * NC + c
                first = isinstance(g, int) and n == 0
                left, made = conv_tiles(g, last, c)
                splits = () if last else SPLIT_IN.get(c, ())
                for T, tg, j, _ in left:
                    tile_in(T, tg, j)
                act.wait_ge(s_xt, n + 1)
                wait(act, s_xd, n - 1)
                act.activation(xs[:, c % 2, :], p_x[:], ACT.Copy).then_inc(s_xs, 1)
                if not first:
                    z_round(n - 1)
                act.wait_ge(s_d, n + 1)
                wait(act, s_intra, n - 1)
                for k, p in enumerate((p_d0, p_d1)):
                    act.activation(em[:, c % 2, k * 512:(k + 1) * 512], p[:], ACT.Exp).then_inc(s_e, 1)
                for T, tg, j, _ in left:
                    tile_tanh(T, j)
                if c == NC - 1 and not last:
                    act.wait_ge(s_gate, n + 1)
                for w in splits[:2]:
                    w_round(g + 1, w)
                for T, tg, j, _ in made[:1]:
                    tile_in(T, tg, j)
                    if not left:
                        tile_tanh(T, j)
                if c == 0:
                    wait(act, s_out, n)
                    w_round(g, TILES + KT)
                    w_round(g, TILES + KT + 1)
                for w in splits[2:]:
                    w_round(g + 1, w)
                act.wait_ge(s_y, n + 1)
                wait(act, s_ss, n)
                wait(act, s_v, n - 1)
                act.activation(junk[:], y[:, c % 2, :], ACT.Square, accum_out=ss[:, c % 2:c % 2 + 1])\
                    .then_inc(s_ss, 1)
                if left:
                    for T, tg, j, _ in made[:1]:
                        tile_tanh(T, j)
                if not (last and c == NC - 1):
                    gate_tanh(n + 1)
                if c == 0:
                    w_round(g, TILES + KT + 2)
                    w_round(g, TILES + KT + 3)

        w_round(0, 0)
        w_round(0, 1)
        for c in range(NC):
            act.wait_ge(ln_tr, c + 1)
            act.activation(xn_hi[:, :, c * P:(c + 1) * P], (p_x, p_in)[c % 2][:].rearrange("p (k t) -> p k t", k=KT),
                           ACT.Copy).then_inc(ln_hi, 1)
        act.wait_ge(s_halved, 2)
        w_round(0, 2)
        w_round(0, 3)
        act.wait_ge(dt_ve, 4)
        act.activation(t_e, t_v, ACT.Abs).then_inc(dt_ac, 1)
        act.wait_ge(dt_ac, 1)
        act.activation(t_e, t_e, ACT.Exp, scale=-1.0).then_inc(dt_ac, 1)
        act.activation(head_c[:, 3:4], head_c[:, 1:2], ACT.Exp).then_inc(dt_ac, 1)
        w_round(0, 4)
        w_round(0, 5)
        act.wait_ge(dt_ve, 5)
        act.activation(t_r, t_w, ACT.Ln).then_inc(dt_ac, 1)
        for w in range(6, TILES + KT):
            w_round(0, w)
        act.wait_ge(dt_tp, 4)
        act.activation(ecum_t[:].rearrange("p c h -> p (c h)"), p_y[:], ACT.Exp).then_inc(dt_ac, 1)
        act.activation(dtw_t[:].rearrange("p c h -> p (c h)"), p_gb[:], ACT.Exp).then_inc(dt_ac, 1)
        act.activation(etot_t[:].rearrange("p c h -> p (c h)"), p_d0[:], ACT.Exp).then_inc(dt_ac, 1)
        act.wait_ge(dt_ve, 15)
        for j in range(TILES):
            tile_in(j, 0, j)
            tile_tanh(j, j)
        gate_tanh(0)
        group(0, False)
        with act.Fori(1, G - 1) as g:
            group(g, False)
        group(G - 1, True)
        z_round(LAST)

    @block.vector
    def _(ve):
        def first_taps(T, g, j, hf):
            s = j % 2
            wait(ve, s_tap, TAPS * (T - 1))
            if hf == 0:
                ve.memset(pre[:, s, 0:TAPS - 1], 0.0).then_inc(s_halo, 1)
            else:
                ve.tensor_copy(pre[:, s, 0:TAPS - 1], halo[:, j, :]).then_inc(s_halo, 1)
            ve.wait_ge(s_cin, 2 * (T + 1))
            ve.wait_ge(s_halo, T + 1)
            for k in range(TAPS - 2):
                tap(T, g, j, k)

        def tap(T, g, j, k):
            s = j % 2
            wait(ve, s_tap, TAPS * T + k)
            ve.scalar_tensor_tensor(out=conv[:, s, :], in0=pre[:, s, k:k + HALF],
                                    scalar=conv_w[:, bass.ds(g, 1), j, k],
                                    in1=conv[:, s, :], op0=ALU.mult, op1=ALU.add).then_inc(s_tap, 1)

        def last_tap(T, g, j, hf):
            tap(T, g, j, TAPS - 2)
            ve.tensor_copy(halo[:, j, :], pre[:, j % 2, HALF:HALF + TAPS - 1]).then_inc(s_tap, 1)

        def silu(T, g, j, hf):
            ve.wait_ge(s_th, T + 1)
            ve.scalar_tensor_tensor(out=xbc[:, j, half_cols(hf)], in0=conv_th[:, j % 2, :], scalar=1.0,
                                    in1=conv[:, j % 2, :], op0=ALU.add, op1=ALU.mult).then_inc(s_xc, 1)

        def variance(m, slot):
            ve.wait_ge(s_ss, m + 1)
            wait(ve, s_rs, m - 1)
            ve.tensor_scalar(ssv[:, slot:slot + 1], ss[:, slot:slot + 1], 1.0 / GW, EPS, ALU.mult, ALU.add)\
                .then_inc(s_v, 1)

        def z_rest(m):
            ve.wait_ge(s_zhi, m + 1)
            ve.tensor_tensor(zt_lo[:].rearrange("p k t -> p (k t)"), p_in[:],
                             zt_hi[:].rearrange("p k t -> p (k t)").bitcast(F32), ALU.subtract).then_inc(s_zlo, 1)

        def residual(m, c):
            ve.wait_ge(s_out, m + 1)
            ve.wait_ge(s_rs, m + 1)
            wait(ve, s_res, m)
            ve.scalar_tensor_tensor(out=x_res[:, c, :], in0=p_y[:], scalar=g_rstd[:, c % 2:c % 2 + 1],
                                    in1=x_res[:, c, :], op0=ALU.mult, op1=ALU.add).then_inc(s_res, 1)

        def gate_silu(m):
            ve.wait_ge(s_tg, m + 1)
            wait(ve, s_z, m)
            ve.scalar_tensor_tensor(out=gate[:], in0=gate_th[:], scalar=1.0, in1=p_gate[:],
                                    op0=ALU.add, op1=ALU.mult).then_inc(s_sg, 1)

        def w_rest(g, w):
            k = w - TILES - KT
            ve.wait_ge(s_whi, g * WT + w + 1)
            ve.scalar_tensor_tensor(out=w_lo[:, w, :], in0=w_raw[:, w % 2, :], scalar=norm_w[:, bass.ds(g, 1), k],
                                    in1=w_hi[:, w, :].bitcast(F32), op0=ALU.mult, op1=ALU.subtract)\
                .then_inc(s_wloo, 1)

        def group(g, last):
            wait(ve, s_xd, g * NC)
            wait(ve, s_t, g * (NC - 1))
            for k, a in enumerate((dt_t, dtw_t, ecum_t, etot_t)):
                ve.tensor_scalar(head_g[:, k, :, :], a[:, :, bass.ds(g * HG, HG)], 1.0, None, ALU.mult)\
                    .then_inc(s_head, 1)
            ve.tensor_scalar(d_g[:], d_b[:, bass.ds(g * HG, HG)], 1.0, None, ALU.mult).then_inc(s_head, 1)
            for c in range(NC):
                n = g * NC + c
                st = g * (NC - 1) + c
                first = isinstance(g, int) and n == 0
                left, made = conv_tiles(g, last, c)
                made = made[:1]
                if not first:
                    variance(n - 1, (c - 1) % 2)
                ve.wait_ge(s_gb, n + 1)
                wait(ve, s_gm, 2 * n)
                wait(ve, s_m, 2 * n)
                ve.tensor_tensor(gm[:], p_gb[:, 0:P], tri[:], ALU.mult).then_inc(s_gm, 1)
                ve.tensor_copy(b_tok[:], p_gb[:, P:2 * P]).then_inc(s_gm, 1)
                if not first:
                    z_rest(n - 1)
                ve.wait_ge(s_gm, 2 * (n + 1))
                for k in range(2):
                    ve.wait_ge(s_e, 2 * n + k + 1)
                    m = em[:, c % 2, k * 512:(k + 1) * 512].rearrange("p (h t) -> p h t", h=HG // 2)
                    ve.tensor_tensor(m, m, gm[:].unsqueeze(1).broadcast_to([P, HG // 2, P]), ALU.mult)\
                        .then_inc(s_m, 1)
                for tile in left:
                    first_taps(*tile)
                    last_tap(*tile)
                if not left:
                    for tile in made:
                        first_taps(*tile)
                if not first:
                    residual(n - 1, (c - 1) % NC)
                for tile in left:
                    silu(*tile)
                if not left:
                    for tile in made:
                        last_tap(*tile)
                if c > 0:
                    ve.wait_ge(s_inter, st)
                    ve.wait_ge(s_head, 5 * (g + 1))
                    wait(ve, s_ss, n - 1)
                    wait(ve, s_z, n - 1)
                    ve.tensor_tensor(by_head(y[:, c % 2, :]), by_head(p_in[:]), heads(ECUM, c), ALU.mult)\
                        .then_inc(s_t, 1)
                ve.wait_ge(s_stn, n + 1)
                wait(ve, s_stu, n)
                if c > 0:
                    ve.wait_ge(s_std, st)
                    ve.tensor_tensor(state[:], p_x[:], state_dec[:], ALU.add).then_inc(s_stu, 1)
                else:
                    ve.tensor_copy(state[:], p_x[:]).then_inc(s_stu, 1)
                for tile in made:
                    if left:
                        first_taps(*tile)
                    else:
                        silu(*tile)
                if c == 0:
                    w_rest(g, TILES + KT)
                    w_rest(g, TILES + KT + 1)
                ve.wait_ge(s_intra, n + 1)
                if c > 0:
                    ve.wait_ge(s_txd, st)
                    ve.tensor_tensor(y[:, c % 2, :], y[:, c % 2, :], p_y[:], ALU.add).then_inc(s_y, 1)
                else:
                    ve.wait_ge(s_xd, n + 1)
                    wait(ve, s_ss, n - 1)
                    wait(ve, s_z, n - 1)
                    ve.tensor_tensor(y[:, c % 2, :], x_d[:], p_y[:], ALU.add).then_inc(s_y, 1)
                ve.wait_ge(s_y, n + 1)
                ve.wait_ge(s_sg, n + 1)
                wait(ve, s_zt, n)
                ve.tensor_tensor(z[:], y[:, c % 2, :], gate[:], ALU.mult).then_inc(s_z, 1)
                if left:
                    for tile in made:
                        last_tap(*tile)
                        silu(*tile)
                if not (last and c == NC - 1):
                    gate_silu(n + 1)
                if c == 0:
                    w_rest(g, TILES + KT + 2)
                    w_rest(g, TILES + KT + 3)

        for c in range(NC):
            ve.wait_ge(s_x[c], 16)
            ve.bn_stats(stats[:, c, :], x_res[:, c, :]).then_inc(ln_st, 1)
            ve.wait_ge(ln_st, c + 1)
            ve.bn_aggr(mean_var[:, c, :], stats[:, c, :]).then_inc(ln_var, 1)
        ve.wait_ge(ln_var, NC)
        ve.tensor_scalar(rstd[:], mean_var[:, :, 1], EPS, None, ALU.add).then_inc(ln_var, 1)
        ve.wait_ge(s_const, 16 * 7)
        ve.tensor_scalar(conv_w[:], conv_w[:], 0.5, None, ALU.mult).then_inc(s_halved, 1)
        ve.tensor_scalar(norm_w[:], norm_w[:], 0.5, None, ALU.mult).then_inc(s_halved, 1)
        ve.tensor_copy(w_hi[:, WT - 1, :], z[:]).then_inc(ln_st, 1)
        ve.wait_ge(ln_st, NC + 1)
        ve.tensor_tensor(w_lo[:, WT - 1, :], z[:], w_hi[:, WT - 1, :].bitcast(F32), ALU.subtract)\
            .then_inc(dt_ve, 1)
        ve.wait_ge(ln_rs, 2)

        def ln_rest(c):
            ve.wait_ge(ln_hi, c + 1)
            ve.tensor_tensor(xn_lo[:, :, c * P:(c + 1) * P], (p_x, p_in)[c % 2][:].rearrange("p (k t) -> p k t", k=KT),
                             xn_hi[:, :, c * P:(c + 1) * P].bitcast(F32), ALU.subtract).then_inc(ln_lo, 1)

        for c in range(NC):
            wait(ve, ln_tr, c - 1)
            ve.tensor_scalar(xnt[:, c % 2, :], x_res[:, c, :], mean_var[:, c, 0:1], rstd[:, c:c + 1],
                             ALU.subtract, ALU.mult).then_inc(ln_xn, 1)
            if c > 0:
                ln_rest(c - 1)
        ln_rest(NC - 1)
        for a in range(2):
            ve.wait_ge(dt_mm, a + 1)
            ve.tensor_scalar(t_v[:, a, :], (p_d0, p_d1)[a][0:H, :], head_c[0:H, 0:1], None, ALU.add).then_inc(dt_ve, 1)
        ve.memset(t_mask, 1.0).then_inc(dt_ve, 1)
        ve.wait_ge(dt_ac, 2)
        ve.tensor_scalar(t_w, t_e, 1.0, None, ALU.add).then_inc(dt_ve, 1)
        ve.wait_ge(dt_ve, 5)
        ve.tensor_scalar(t_dt, t_w, -1.0, None, ALU.add).then_inc(dt_ve, 1)
        ve.reciprocal(t_rem, t_w).then_inc(dt_ve, 1)
        ve.wait_ge(dt_ve, 7)
        ve.tensor_tensor(t_dt, t_e, t_dt, ALU.subtract).then_inc(dt_ve, 1)
        ve.wait_ge(dt_ve, 8)
        ve.tensor_tensor(t_dt, t_dt, t_rem, ALU.mult).then_inc(dt_ve, 1)
        ve.wait_ge(dt_ve, 9)
        ve.wait_ge(dt_ac, 4)
        ve.tensor_tensor(t_dt, t_dt, t_r, ALU.add).then_inc(dt_ve, 1)
        ve.tensor_scalar(t_v, t_v, 0.0, None, ALU.max).then_inc(dt_ve, 1)
        ve.wait_ge(dt_ve, 11)
        ve.tensor_tensor(t_dt, t_dt, t_v, ALU.add).then_inc(ln_st, 1)
        ve.tensor_scalar(head_c[:, 2:3], head_c[:, 3:4], -1.0, None, ALU.mult).then_inc(ln_st, 1)
        ve.memset(t_mask[:, :, 0:HALF:P], 0.0).then_inc(ln_st, 1)
        ve.wait_ge(ln_st, NC + 4)
        ve.tensor_scalar(t_a, t_dt, head_c[0:H, 2:3], LOG_FLOOR, ALU.mult, ALU.max).then_inc(ln_st, 1)
        ve.wait_ge(ln_st, NC + 5)
        for a in range(2):
            ve.tensor_tensor_scan(t_cum[:, a, :], t_mask[:, a, :], t_a[:, a, :], 0.0, ALU.mult, ALU.add)\
                .then_inc(ln_st, 1)
        ve.wait_ge(ln_st, NC + 7)
        cum_c = t_cum.rearrange("p a (c t) -> p (a c) t", t=P)
        ve.tensor_tensor(t_rem.rearrange("p a (c t) -> p (a c) t", t=P), cum_c[:, :, P - 1:P].broadcast_to([H, NC, P]),
                         cum_c, ALU.subtract).then_inc(dt_ve, 1)
        ve.tensor_copy(t_parts[0], t_cum).then_inc(dt_ve, 1)
        ve.wait_ge(dt_ve, 13)
        ve.tensor_tensor(t_r, t_cum, t_parts[0], ALU.subtract).then_inc(ln_st, 1)
        ve.wait_ge(ln_st, NC + 8)
        ve.tensor_copy(t_parts[1], t_r).then_inc(dt_ve, 1)
        ve.wait_ge(dt_ve, 14)
        ve.tensor_tensor(t_parts[2], t_r, t_parts[1], ALU.subtract).then_inc(dt_ve, 1)
        ve.wait_ge(dt_tp, 4)
        ve.tensor_copy(dt_t[:].rearrange("p c h -> p (c h)"), p_gate[:]).then_inc(dt_ve, 1)
        ve.wait_ge(dt_ac, 7)
        ve.wait_ge(dt_ve, 16)
        ve.tensor_tensor(dtw_t[:], dtw_t[:], dt_t[:], ALU.mult).then_inc(dt_ve, 1)
        for j in range(TILES):
            first_taps(j, 0, j, 0)
            last_tap(j, 0, j, 0)
            silu(j, 0, j, 0)
        gate_silu(0)
        group(0, False)
        with ve.Fori(1, G - 1) as g:
            group(g, False)
        group(G - 1, True)
        variance(LAST, (NC - 1) % 2)
        z_rest(LAST)
        residual(LAST, NC - 1)

    @block.tensor
    def _(pe):
        def conv_tile(T, g, j, hf):
            wait(pe, s_cin, 2 * T)
            if hf == 0:
                pe.wait_ge(s_whi, g * WT + j + 1)
                pe.wait_ge(s_wlo, g * (TILES + KT) + j + 1)
            three_pass(pe, p_tile[:],
                       lambda k: (w_hi[:, j, k * P:(k + 1) * P], w_lo[:, j, k * P:(k + 1) * P]),
                       lambda k: (xn_hi[:, k, half_cols(hf)], xn_lo[:, k, half_cols(hf)]), KT).then_inc(s_prj, 1)

        def z_transpose(m):
            pe.wait_ge(s_z, m + 1)
            for k in range(GW // P):
                mm = pe.transpose(p_in[:, k * P:(k + 1) * P], z[:, k * P:(k + 1) * P], ident[:])
            mm.then_inc(s_zt, 1)

        def gate_product(m, c):
            wait(pe, s_sg, m)
            cs = slice(c * P, (c + 1) * P)
            three_pass(pe, p_gate[:], lambda k: (xn_hi[:, k, cs], xn_lo[:, k, cs]),
                       lambda k: (w_hi[:, TILES + k, :], w_lo[:, TILES + k, :]), KT).then_inc(s_gate, 1)

        def out_product(m):
            pe.wait_ge(s_zlo, m + 1)
            three_pass(pe, p_y[:], lambda k: (zt_hi[:, k, :], zt_lo[:, k, :]),
                       lambda k: (w_hi[:, TILES + KT + k, :], w_lo[:, TILES + KT + k, :]), GW // P).then_inc(s_out, 1)

        def group(g, last):
            for c in range(NC):
                n = g * NC + c
                first = isinstance(g, int) and n == 0
                left, made = conv_tiles(g, last, c)
                cs = slice(c * P, (c + 1) * P)
                if c % CH == 0:
                    pe.wait_ge(s_xc, (2 * g + c // CH + 1) * TILES)
                wait(pe, s_stu, n)
                for j in range(GW // P):
                    mm = pe.transpose(p_x[:, j * P:(j + 1) * P], xbc[:, j, cs], ident[:])
                mm.then_inc(s_xt, 1)
                wait(pe, s_gm, 2 * n)
                pe.transpose(p_gb[:, P:2 * P], xbc[:, TB, cs], ident[:])
                pe.matmul(p_gb[:, 0:P], xbc[:, TB, cs], xbc[:, TC, cs], start=True, stop=True).then_inc(s_gb, 1)
                pe.wait_ge(s_dl[c % 2], 32 * (g * (NC // 2) + c // 2 + 1))
                wait(pe, s_e, 2 * n)
                for k, p in enumerate((p_d0, p_d1)):
                    mm = pe.matmul(p[:], d_lhs[:, c % 2, :], d_rhs[:, c % 2, k * 512:(k + 1) * 512],
                                   start=True, stop=True)
                mm.then_inc(s_d, 1)
                if not first:
                    z_transpose(n - 1)
                for tile in made[:1]:
                    conv_tile(*tile)
                if c == 1:
                    pe.wait_ge(s_whi, (g + 1) * WT)
                    pe.wait_ge(s_wloo, (g + 1) * (GW // P))
                if not first:
                    out_product(n - 1)
                if c > 0:
                    pe.wait_ge(s_stu, n)
                    pe.wait_ge(s_zlo, n)
                    pe.matmul(p_in[:], xbc[:, TC, cs], state[:], start=True, stop=True).then_inc(s_inter, 1)
                pe.wait_ge(s_gm, 2 * (n + 1))
                pe.wait_ge(s_xw, n + 1)
                pe.wait_ge(s_xs, n + 1)
                pe.matmul(p_x[:], b_tok[:], x_w[:], start=True, stop=True).then_inc(s_stn, 1)
                pe.wait_ge(s_m, 2 * (n + 1))
                pe.wait_ge(s_xdt, n + 1)
                wait(pe, s_res, n)
                for h in range(HG):
                    mm = pe.matmul(p_y[:, h * HD:(h + 1) * HD], em[:, c % 2, h * P:(h + 1) * P],
                                   x_dt[:, h * HD:(h + 1) * HD], start=True, stop=True)
                mm.then_inc(s_intra, 1)
                if c + 1 < NC:
                    gate_product(n + 1, c + 1)
                elif not last:
                    pe.wait_ge(s_whi, (g + 1) * WT + TILES + KT)
                    pe.wait_ge(s_wlo, (g + 2) * (TILES + KT))
                    gate_product(n + 1, 0)
                for tile in made[1:]:
                    conv_tile(*tile)

        pe.wait_ge(s_const, 16 * 7)
        for c in range(NC):
            pe.wait_ge(ln_xn, c + 1)
            wait(pe, ln_lo, c - 1)
            for k in range(KT):
                mm = pe.transpose((p_x, p_in)[c % 2][:, k * P:(k + 1) * P], xnt[:, c % 2, k * P:(k + 1) * P], ident[:])
            mm.then_inc(ln_tr, 1)
        pe.wait_ge(dt_ve, 1)
        for a in range(2):
            pe.wait_ge(ln_lo, CH * (a + 1))
            three_pass(pe, (p_d0, p_d1)[a][:],
                       lambda k: (w_hi[:, WT - 1, k * P:(k + 1) * P], w_lo[:, WT - 1, k * P:(k + 1) * P]),
                       lambda k: (xn_hi[:, k, half_cols(a)], xn_lo[:, k, half_cols(a)]), KT).then_inc(dt_mm, 1)
        conv_tile(0, 0, 0, 0)
        pe.wait_ge(dt_ve, 12)
        for src, dst in ((t_dt, p_gate), (t_cum, p_y), (t_rem, p_gb), (None, p_d0)):
            for c in range(NC):
                a, b = c // CH, (c % CH) * P
                rows_c = src[:, a, b:b + P] if src is not None \
                    else t_cum[:, a, b + P - 1:b + P].broadcast_to([H, P])
                mm = pe.transpose(dst[:, c * H:(c + 1) * H], rows_c, ident[0:H, 0:H])
            mm.then_inc(dt_tp, 1)
        for j in range(1, TILES):
            conv_tile(j, 0, j, 0)
        pe.wait_ge(s_whi, TILES + KT)
        pe.wait_ge(s_wlo, TILES + KT)
        gate_product(0, 0)
        group(0, False)
        with pe.Fori(1, G - 1) as g:
            group(g, False)
        group(G - 1, True)
        z_transpose(LAST)
        out_product(LAST)


INTER = 1376
GRP = 128
NT = -(-INTER // P)
GU = D // GRP
GD = INTER // GRP
NI = NT * P


def swiglu_up(nc, io, ctx, x_res, h, wd_hi, wd_lo, ident):
    def sb(name, shape, dt=F32):
        return ctx.enter_context(nc.sbuf_tensor(name, shape, dt))

    def pb(name):
        return ctx.enter_context(nc.psum_tensor(name, [P, 512], F32))

    def sem(name):
        return ctx.enter_context(nc.semaphore(name))

    xn_hi = sb("f_xn_hi", [P, KT, L], F32R)
    xn_lo = sb("f_xn_lo", [P, KT, L], F32R)
    q = sb("q_words", [P, 3, 512], I32)
    q4 = sb("q4", [P, 2, 512], I32)
    wz = sb("wz", [P, 2, 512])
    wf = sb("wf", [P, 2, 512])
    w_hi = sb("f_w_hi", [P, 2, 512], F32R)
    w_lo = sb("f_w_lo", [P, 2, 512], F32R)
    g_th = sb("g_th", [P, 2, HALF])
    g_act = sb("g_act", [P, 2, HALF])
    rows = sb("f_rows", [P, 2, D])
    shift = sb("q_shift", [P, 1], I32)
    sc_gu = sb("sc_gu_parts", [PART * GU, 2 * NI], BF16)
    sc_d = sb("sc_d_parts", [P, D], BF16)
    zp_gu = sb("zp_gu", [GU, 2 * NI], BF16)
    zp_d = sb("zp_d", [P, D], BF16)
    hot_gu = sb("hot_gu", [PART * GU, 2 * D], BF16)
    hot_d = sb("hot_d", [P, NI], BF16)
    row_of = sb("row_groups", [PART * GD, 2])
    NSC = 2 * GU * NI // P
    NSD = GD * D // P
    sc_raw = sb("sc_raw", [P, NSC + NSD])
    sc_rest = sb("sc_rest", [P, NSC + NSD])
    sc_part = [sb(f"sc_part{k}", [P, NSC + NSD], BF16) for k in range(PART)]
    stats = sb("f_stats", [P, NC, 6])
    mean_var = sb("f_mean_var", [P, NC, 2])
    rstd = sb("f_rstd", [P, NC])
    m_half = sb("f_m_half", [P, 1])
    gi_gu = wz[0:PART * GU, :, :].rearrange("p a n -> p (a n)").bitcast(I32)
    gi_d0 = g_act[0:PART * GD, :, :].rearrange("p a n -> p (a n)").bitcast(I32)
    gi_d1 = g_th[0:PART * GD, 0, 0:NI - L].bitcast(I32)
    zq_gu = wf[0:GU, 0, 0:2 * NI // 8].bitcast(I32)
    zq_d = wf[0:GD, 1, 0:D // 8].bitcast(I32)
    z4_gu = q4[0:GU, 0, 0:2 * NI // 8]
    z4_d = q4[0:GD, 1, 0:D // 8]

    p_z, p_s, p_g, p_u = ([pb(f"p_{k}{i}") for i in range(2)] for k in "zsgu")
    sc_dram = nc.dram_tensor("sc_parts", [PART, P, NSC], BF16, kind="Internal").ap()
    sd_dram = nc.dram_tensor("sd_parts", [PART, P, NSD], BF16, kind="Internal").ap()

    f_zero = sem("f_zero")
    f_small, f_gi, f_sc, f_sc2, f_zp, f_split = (sem(f"f_{k}") for k in ("small", "gi", "sc", "sc2", "zp", "split"))
    ln_st, ln_var, ln_rs, ln_xn, ln_tr, ln_hi, ln_lo = (sem(f"fln_{k}") for k in "abcdefg")
    s_q = [sem(f"f_q{m}") for m in range(3)]
    s_dq, s_g, s_u = (sem(f"f_pe_{k}") for k in ("dq", "g", "u"))
    s_unp, s_wz, s_wf, s_ga, s_h = (sem(f"f_ve_{k}") for k in ("unp", "wz", "wf", "ga", "h"))
    s_hi, s_th, s_lo, s_lod = sem("f_act_hi"), sem("f_act_th"), sem("f_pool_lo"), sem("f_ve_lod")

    q_rows = io["q"].rearrange("u p n -> (u p) n")
    block = ctx.enter_context(nc.Block())
    LAST_T = NT - 1

    def is_last(t):
        return isinstance(t, int) and t == LAST_T

    def dest(wd, w, t, m):
        return wd[:, bass.ds(t, 1), :].rearrange("p a n -> p (a n)") if m == 2 else w[:, m, :]

    def both_tiles(eng, tile):
        tile(0, 0)
        tile(1, 1)
        with eng.Fori(1, NT // 2) as i:
            tile(2 * i, 0)
            tile(2 * i + 1, 1)
        tile(LAST_T, LAST_T % 2)

    def half_of(hf):
        return slice(hf * HALF, (hf + 1) * HALF)

    @block.sync
    def _(sp):
        def load_q(t, m):
            row = at(sp, (3 * t + m) * P)
            wait(sp, s_unp, 3 * t + m - 2)
            sp.dma_start(q[:, m, :], q_rows[bass.ds(row, P), :]).then_inc(s_q[m], 16)

        sp.dma_start(sc_raw[:, 0:NSC], io["sc_gu"]).then_inc(f_small, 16)
        sp.dma_start(sc_raw[:, NSC:], io["sc_d"]).then_inc(f_small, 16)
        sp.dma_start(shift[:], io["shift"]).then_inc(f_small, 16)
        sp.dma_start(row_of[:], io["row_of"]).then_inc(f_small, 16)
        sp.dma_start(zq_gu, io["zq_gu"]).then_inc(f_small, 16)
        sp.dma_start(zq_d, io["zq_d"]).then_inc(f_small, 16)
        sp.dma_start(gi_gu, io["gi_gu"].broadcast_to([PART * GU, 2 * D])).then_inc(f_gi, 16)
        sp.dma_start(gi_d0, io["gi_d"][:, 0:L].broadcast_to([PART * GD, L])).then_inc(f_gi, 16)
        sp.dma_start(gi_d1, io["gi_d"][:, L:NI].broadcast_to([PART * GD, NI - L])).then_inc(f_gi, 16)
        for m in range(3):
            load_q(0, m)
        for k in range(PART):
            sp.wait_ge(f_split, 2 * k + 1)
            sp.dma_start(sc_dram[k], sc_part[k][:, 0:NSC]).then_inc(f_sc, 16)
            sp.dma_start(sd_dram[k], sc_part[k][:, NSC:]).then_inc(f_sc, 16)
        sp.wait_ge(f_sc, 32 * PART)
        sp.wait_ge(f_zero, 1)
        sp.dma_start(sc_gu[:], sc_dram.rearrange("k p n -> (k p n)").rearrange("(r n) -> r n", n=2 * NI))\
            .then_inc(f_sc2, 16)
        sp.dma_start(sc_d[0:PART * GD, :], sd_dram.rearrange("k p n -> (k p n)").rearrange("(r n) -> r n", n=D)).then_inc(f_sc2, 16)
        for m in range(3):
            load_q(1, m)
        with sp.Fori(2, NT) as t:
            for m in range(3):
                load_q(t, m)

    @block.gpsimd
    def _(pool):
        def rest(t, m, slot):
            pool.wait_ge(s_hi, 3 * t + m + 1)
            pool.tensor_tensor(w_lo[:, m, :], wf[:, slot, :], w_hi[:, m, :].bitcast(F32), ALU.subtract)\
                .then_inc(s_lo, 1)

        pool.memset(m_half[:], -0.5).then_inc(ln_rs, 1)
        for a in (sc_d, zp_d, hot_d):
            pool.memset(a[:], 0.0).then_inc(f_zero, 1)
        pool.wait_ge(ln_var, NC + 1)
        pool.wait_ge(ln_rs, 1)
        pool.tensor_tensor(rstd[:], rstd[:], m_half[:].broadcast_to([P, NC]), ALU.pow).then_inc(ln_rs, 1)
        rest(0, 0, 0)
        rest(0, 1, 1)

        def tile(t, odd):
            if not is_last(t):
                rest(t + 1, 0, 1 - odd)
                rest(t + 1, 1, odd)

        both_tiles(pool, tile)

    @block.scalar
    def _(act):
        def round_w(t, m, slot):
            u = 3 * t + m
            act.wait_ge(s_wf, u + 1)
            if m < 2:
                wait(act, (s_g, s_u)[m], 2 * t)
            act.activation(dest(wd_hi, w_hi, t, m), wf[:, slot, :], ACT.Copy).then_inc(s_hi, 1)

        def tanh(t, hf):
            act.wait_ge(s_g, 2 * t + hf + 1)
            wait(act, s_ga, 2 * t + hf - 1)
            act.activation(g_th[:, hf, :], p_g[hf][:], ACT.Tanh, scale=0.5).then_inc(s_th, 1)

        for c in range(NC):
            act.wait_ge(ln_tr, c + 1)
            act.activation(xn_hi[:, :, c * P:(c + 1) * P], p_g[c % 2][:].rearrange("p (k t) -> p k t", k=KT),
                           ACT.Copy).then_inc(ln_hi, 1)
        round_w(0, 0, 0)
        round_w(0, 1, 1)

        def tile(t, odd):
            round_w(t, 2, odd)
            tanh(t, 0)
            tanh(t, 1)
            if not is_last(t):
                round_w(t + 1, 0, 1 - odd)
                round_w(t + 1, 1, odd)

        both_tiles(act, tile)

    @block.vector
    def _(ve):
        def dequant(t, m, slot):
            u = 3 * t + m
            ve.wait_ge(s_q[m], 16 * (t + 1))
            wait(ve, s_wz, u - 1)
            ve.tensor_scalar(q4[:, slot, :], q[:, m, :], shift[:, 0:1], 15, ALU.logical_shift_right,
                             ALU.bitwise_and).then_inc(s_unp, 1)
            ve.wait_ge(s_dq, u + 1)
            ve.wait_ge(s_unp, u + 1)
            wait(ve, s_wf, u - 1)
            ve.tensor_tensor(wz[:, slot, :], q4[:, slot, :], p_z[slot][:], ALU.subtract).then_inc(s_wz, 1)
            ve.wait_ge(s_wz, u + 1)
            if m == 1:
                wait(ve, s_lod, t)
            else:
                wait(ve, s_lo, 2 * t + m // 2)
            ve.tensor_tensor(wf[:, slot, :], wz[:, slot, :], p_s[slot][:], ALU.mult).then_inc(s_wf, 1)

        ve.wait_ge(f_small, 96)
        src = sc_raw
        for k in range(PART):
            wait(ve, f_split, 2 * k)
            ve.tensor_copy(sc_part[k][:], src[:]).then_inc(f_split, 1)
            if k < PART - 1:
                ve.wait_ge(f_split, 2 * k + 1)
                ve.tensor_tensor(sc_rest[:], src[:], sc_part[k][:], ALU.subtract).then_inc(f_split, 1)
            src = sc_rest
        ve.wait_ge(f_gi, 48)
        ve.wait_ge(f_zero, 3)
        n = 0
        for gi, hot, groups, col in ((gi_gu, hot_gu[:], GU, 0), (gi_d0, hot_d[0:PART * GD, 0:L], GD, 1),
                                     (gi_d1, hot_d[0:PART * GD, L:NI], GD, 1)):
            below = rows[0:hot.shape[0], :, :].rearrange("p a n -> p (a n)")[:, 0:hot.shape[1]]
            wait(ve, f_zp, n)
            ve.tensor_scalar(below, gi, 0.0, float(groups), ALU.is_lt, ALU.mult).then_inc(f_zp, 1)
            ve.wait_ge(f_zp, n + 1)
            ve.tensor_tensor(below, below, gi, ALU.add).then_inc(f_zp, 1)
            ve.wait_ge(f_zp, n + 2)
            ve.tensor_scalar(below, below, 0.0, float(groups - 1), ALU.max, ALU.min).then_inc(f_zp, 1)
            ve.wait_ge(f_zp, n + 3)
            ve.tensor_scalar(hot, below, row_of[0:hot.shape[0], col:col + 1], None, ALU.is_equal).then_inc(f_zp, 1)
            n += 4
        for zq, z4, zp in ((zq_gu, z4_gu, zp_gu[:]), (zq_d, z4_d, zp_d[0:GD, :])):
            for i in range(8):
                wait(ve, f_zp, n)
                ve.tensor_scalar(z4, zq, 4 * i, 15, ALU.logical_shift_right, ALU.bitwise_and).then_inc(f_zp, 1)
                ve.wait_ge(f_zp, n + 1)
                ve.tensor_scalar(zp.rearrange("g (c i) -> g c i", i=8)[:, :, i], z4, 1.0, None, ALU.add)\
                    .then_inc(f_zp, 1)
                n += 2
        ve.wait_ge(f_zp, n)
        for c in range(NC):
            ve.bn_stats(stats[:, c, :], x_res[:, c, :]).then_inc(ln_st, 1)
        for c in range(NC):
            ve.wait_ge(ln_st, c + 1)
            ve.bn_aggr(mean_var[:, c, :], stats[:, c, :]).then_inc(ln_var, 1)
        ve.wait_ge(ln_var, NC)
        ve.tensor_scalar(rstd[:], mean_var[:, :, 1], EPS, None, ALU.add).then_inc(ln_var, 1)
        ve.wait_ge(ln_rs, 2)

        def ln_rest(c):
            ve.wait_ge(ln_hi, c + 1)
            ve.tensor_tensor(xn_lo[:, :, c * P:(c + 1) * P], p_g[c % 2][:].rearrange("p (k t) -> p k t", k=KT),
                             xn_hi[:, :, c * P:(c + 1) * P].bitcast(F32), ALU.subtract).then_inc(ln_lo, 1)

        for c in range(NC):
            wait(ve, ln_tr, c - 1)
            ve.tensor_scalar(rows[:, c % 2, :], x_res[:, c, :], mean_var[:, c, 0:1], rstd[:, c:c + 1],
                             ALU.subtract, ALU.mult).then_inc(ln_xn, 1)
            if c > 0:
                ln_rest(c - 1)
        ln_rest(NC - 1)
        dequant(0, 0, 0)
        dequant(0, 1, 1)

        def gate(t, hf):
            ve.wait_ge(s_th, 2 * t + hf + 1)
            wait(ve, s_h, 2 * t + hf - 1)
            ve.scalar_tensor_tensor(out=g_act[:, hf, :], in0=g_th[:, hf, :], scalar=1.0, in1=p_g[hf][:],
                                    op0=ALU.add, op1=ALU.mult).then_inc(s_ga, 1)

        def down_rest(t, slot):
            ve.wait_ge(s_hi, 3 * t + 3)
            ve.tensor_tensor(wd_lo[:, bass.ds(t, 1), :].rearrange("p a n -> p (a n)"), wf[:, slot, :],
                             dest(wd_hi, w_hi, t, 2).bitcast(F32), ALU.subtract).then_inc(s_lod, 1)

        def inner(t, hf):
            ve.wait_ge(s_u, 2 * t + hf + 1)
            ve.wait_ge(s_ga, 2 * t + hf + 1)
            ve.scalar_tensor_tensor(out=h[:, bass.ds(t, 1), half_of(hf)].rearrange("p a t -> p (a t)"),
                                    in0=g_act[:, hf, :], scalar=0.5, in1=p_u[hf][:],
                                    op0=ALU.mult, op1=ALU.mult).then_inc(s_h, 1)

        def tile(t, odd):
            dequant(t, 2, odd)
            gate(t, 0)
            gate(t, 1)
            down_rest(t, odd)
            if not is_last(t):
                dequant(t + 1, 0, 1 - odd)
            inner(t, 0)
            if not is_last(t):
                dequant(t + 1, 1, odd)
            inner(t, 1)

        both_tiles(ve, tile)

    @block.tensor
    def _(pe):
        def spread(t, m, slot):
            u = 3 * t + m
            wait(pe, s_wf, u - 1)
            if m == 2:
                rows_t = bass.ds(t * P, P)
                pe.matmul(p_z[slot][:], hot_d[:, rows_t], zp_d[:], start=True, stop=True)
                pe.matmul(p_s[slot][:], hot_d[:, rows_t], sc_d[:], start=True, stop=True).then_inc(s_dq, 1)
                return
            cols = bass.ds(m * NI + t * P, P)
            for k in range(KT):
                r = slice(m * D + k * P, m * D + (k + 1) * P)
                pe.matmul(p_z[slot][:, k * P:(k + 1) * P], hot_gu[0:GU, r], zp_gu[:, cols], start=True, stop=True)
            for k in range(KT):
                r = slice(m * D + k * P, m * D + (k + 1) * P)
                mm = pe.matmul(p_s[slot][:, k * P:(k + 1) * P], hot_gu[:, r], sc_gu[:, cols], start=True, stop=True)
            mm.then_inc(s_dq, 1)

        def product(t, m, hf):
            p, done = ((p_g, s_g), (p_u, s_u))[m]
            wait(pe, (s_ga, s_h)[m], 2 * t + hf - 1)
            if hf == 0:
                pe.wait_ge(s_lo, 2 * t + m + 1)
            three_pass(pe, p[hf][:],
                       lambda k: (w_hi[:, m, k * P:(k + 1) * P], w_lo[:, m, k * P:(k + 1) * P]),
                       lambda k: (xn_hi[:, k, half_of(hf)], xn_lo[:, k, half_of(hf)]), KT).then_inc(done, 1)

        for c in range(NC):
            pe.wait_ge(ln_xn, c + 1)
            wait(pe, ln_lo, c - 1)
            for k in range(KT):
                mm = pe.transpose(p_g[c % 2][:, k * P:(k + 1) * P], rows[:, c % 2, k * P:(k + 1) * P], ident[:])
            mm.then_inc(ln_tr, 1)
        pe.wait_ge(f_zp, 12 + 32)
        pe.wait_ge(f_sc2, 32)
        spread(0, 0, 0)
        spread(0, 1, 1)
        spread(0, 2, 0)
        pe.wait_ge(ln_lo, NC)

        def tile(t, odd):
            product(t, 0, 0)
            product(t, 0, 1)
            if not is_last(t):
                spread(t + 1, 0, 1 - odd)
            product(t, 1, 0)
            if not is_last(t):
                spread(t + 1, 1, odd)
            product(t, 1, 1)
            if not is_last(t):
                spread(t + 1, 2, 1 - odd)

        both_tiles(pe, tile)


DH = 16
HQ = 32
HK = 8
REP = HQ // HK
QW = DH * HK
KVW = DH * HK
QKV = QW + 2 * KVW
D_VE = 11

E = 8
RANK = 16
ER = E * RANK
LORA_SCALE = 2.0


def token_tiles(nc, io, ctx, x_res, h, wd_hi, wd_lo, ident):
    def sb(name, shape, dt=F32):
        return ctx.enter_context(nc.sbuf_tensor(name, shape, dt))

    def pb(name):
        return ctx.enter_context(nc.psum_tensor(name, [P, 512], F32))

    def sem(name):
        return ctx.enter_context(nc.semaphore(name))

    h_hi, h_lo = sb("h_hi", [P, NT, P], F32R), sb("h_lo", [P, NT, P], F32R)
    n2_hi, n2_lo = sb("n2_hi", [P, KT, P], F32R), sb("n2_lo", [P, KT, P], F32R)
    n3_hi, n3_lo = sb("n3_hi", [P, KT, P], F32R), sb("n3_lo", [P, KT, P], F32R)
    hw_hi, hw_lo = sb("hw_hi", [P, P], F32R), sb("hw_lo", [P, P], F32R)
    qkv_hi, qkv_lo = sb("qkv_hi", [P, KT, QKV], F32R), sb("qkv_lo", [P, KT, QKV], F32R)
    wb_hi, wb_lo = sb("wb_hi", [P, KT, D], F32R), sb("wb_lo", [P, KT, D], F32R)
    wa_hi, wa_lo = sb("wa_hi", [P, KT, ER + E], F32R), sb("wa_lo", [P, KT, ER + E], F32R)
    wl_hi, wl_lo = sb("wl_hi", [P, D], F32R), sb("wl_lo", [P, D], F32R)
    prod = sb("prod", [P, DH * DH * HK])
    wq_sum = sb("wq_sum", [P, KT, QW])
    wkv_raw = sb("wkv_raw", [P, KT, 2 * KVW])
    wa_raw = sb("wa_raw", [P, KT, ER + E])
    wl_raw = sb("wl_raw", [P, D])
    b_qkv = sb("b_qkv", [P, QKV])
    b_base = sb("b_base_rows", [P, D])
    rows2, rows3 = sb("rows2", [P, D]), sb("rows3", [P, D])
    qkv = sb("qkv", [P, QKV])
    s = sb("scores", [P, DH, DH])
    mx = sb("score_max", [P, DH])
    den = sb("score_sum", [P, DH])
    o = sb("att_out", [P, DH, HK])
    st2, st3 = sb("t_st2", [P, 6]), sb("t_st3", [P, 6])
    mv2, mv3 = sb("t_mv2", [P, 2]), sb("t_mv3", [P, 2])
    rs2, rs3 = sb("t_rs2", [P, 2]), sb("t_rs3", [P, 2])
    m_half = sb("t_m_half", [P, 1])
    lg, m8, w8, w8b, expert = (sb(f"route_{k}", [P, E]) for k in ("lg", "m8", "w8", "w8b", "iota"))
    i8 = sb("route_i8", [P, E], U32)
    sel = sb("route_sel", [P, 2])
    rt = sb("route_rt", [P, 3])
    hw = sb("hw", [P, ER])
    out_t = sb("out_t", [P, D])
    bq_raw = out_t

    p_a, p_t2, p_t3, p_t4, p_b, p_c, p_r = (pb(f"t_p_{k}") for k in ("a", "t2", "t3", "t4", "b", "c", "r"))

    w_in = [sem(f"t_in{k}") for k in range(4)]
    w_wb, w_sum, w_hi_s, w_lo_s, c_pool = (sem(f"t_{k}") for k in ("wb", "sum", "whi", "wlo", "cpool"))
    s_a, s_t2, s_t3, s_t4, s_b, s_c, s_dl = (sem(f"t_pe_{k}") for k in ("a", "t2", "t3", "t4", "b", "c", "dl"))
    a_h, a_n2, a_n3, a_hw, a_exp, a_rt = (sem(f"t_act_{k}") for k in ("h", "n2", "n3", "hw", "exp", "rt"))
    g_h, g_m1, g_m2, g_rs2, g_rs3, g_xb = (sem(f"t_pool_{k}") for k in ("h", "m1", "m2", "rs2", "rs3", "xb"))
    v_add, v_ln2, v_n2, v_lo2, v_qkv, v_m1, v_s, v_den, v_att, v_x3, v_ln3, v_n3, v_lo3, v_rt, v_hw, v_lo4, v_fin = (
        sem(f"t_ve_{k}") for k in ("add", "ln2", "n2", "lo2", "qkv", "m1", "s", "den", "att", "x3", "ln3",
                                   "n3", "lo3", "rt", "hw", "lo4", "fin"))
    s_store = sem("t_store")

    def flat(ap):
        return ap.rearrange("p a b -> p (a b)")

    def x_tile(c):
        return x_res[:, bass.ds(c, 1), :].rearrange("p a n -> p (a n)")

    def score_product(eng, d0, d1):
        n = d1 - d0
        q = qkv[:, d0 * HK:d1 * HK].rearrange("p (d h) -> p d h", h=HK).unsqueeze(2).broadcast_to([P, n, DH, HK])
        k = qkv[:, QW:QW + KVW].rearrange("p (e h) -> p e h", h=HK).unsqueeze(1).broadcast_to([P, n, DH, HK])
        o4 = prod[:, d0 * DH * HK:d1 * DH * HK].rearrange("p (d e h) -> p d e h", e=DH, h=HK)
        return eng.tensor_tensor(o4, q, k, ALU.mult)

    def value_product(eng, d0, d1):
        n = d1 - d0
        a = s[:, d0:d1, :].unsqueeze(2).broadcast_to([P, n, HK, DH])
        v = qkv[:, QW + KVW:QKV].rearrange("p (e h) -> p h e", h=HK).unsqueeze(1).broadcast_to([P, n, HK, DH])
        o4 = prod[:, d0 * DH * HK:d1 * DH * HK].rearrange("p (d h e) -> p d h e", h=HK, e=DH)
        return eng.tensor_tensor(o4, a, v, ALU.mult)

    def weights():
        return ((qkv_hi[:, :, 0:QW], qkv_lo[:, :, 0:QW], wq_sum[:]),
                (qkv_hi[:, :, QW:], qkv_lo[:, :, QW:], wkv_raw[:]),
                (wa_hi[:], wa_lo[:], wa_raw[:]),
                (wl_hi[:], wl_lo[:], wl_raw[:]),
                (flat(wb_hi[:]), flat(wb_lo[:]), prod[:]))

    def pipeline(step):
        for i in range(NC + 3):
            step(i)

    def live(c):
        return not isinstance(c, int) or 0 <= c < NC

    block = ctx.enter_context(nc.Block())

    @block.sync
    def _(sp):
        sp.dma_start(prod[:], io["wq"]).then_inc(w_in[0], 16)
        sp.dma_start(flat(wkv_raw[:]), io["wkv"]).then_inc(w_in[1], 16)
        sp.dma_start(bq_raw[:], io["bq"].broadcast_to([P, DH * HQ])).then_inc(w_in[2], 16)
        sp.dma_start(b_qkv[:, QW:], io["bkv"].broadcast_to([P, 2 * KVW])).then_inc(w_in[2], 16)
        sp.dma_start(expert[:], io["expert"].broadcast_to([P, E])).then_inc(w_in[2], 16)
        sp.dma_start(b_base[:], io["b_base"].broadcast_to([P, D])).then_inc(w_in[2], 16)
        sp.dma_start(flat(wa_raw[:]), io["wa"]).then_inc(w_in[3], 16)
        sp.dma_start(wl_raw[:], io["wl"]).then_inc(w_in[3], 16)
        sp.wait_ge(w_sum, 1)
        sp.dma_start(prod[:], io["wb"]).then_inc(w_wb, 16)

        def step(i):
            if live(i - 3):
                sp.wait_ge(v_fin, i - 2)
                sp.dma_start(io["out"][bass.ds((i - 3) * P, P), :], out_t[:]).then_inc(s_store, 16)

        pipeline(step)
        sp.wait_ge(s_store, 16 * NC)

    @block.gpsimd
    def _(pool):
        pool.memset(m_half[:], -0.5).then_inc(c_pool, 1)

        def h_rest(c):
            pool.wait_ge(a_h, c + 1)
            pool.tensor_tensor(h_lo[:], h[:, :, bass.ds(c * P, P)], h_hi[:].bitcast(F32), ALU.subtract).then_inc(g_h, 1)

        h_rest(0)
        for n, (hi, lo, raw) in enumerate(weights()):
            pool.wait_ge(w_hi_s, n + 1)
            pool.tensor_tensor(lo, raw, hi.bitcast(F32), ALU.subtract).then_inc(w_lo_s, 1)

        def step(i):
            b, c = i - 1, i - 2
            if live(c):
                pool.wait_ge(a_exp, c + 1)
                pool.wait_ge(v_den, 4 * c + 3)
                value_product(pool, D_VE, DH).then_inc(g_m2, 1)
                pool.wait_ge(v_ln3, 3 * (c + 1))
                pool.tensor_tensor(rs3[:, 1:2], rs3[:, 0:1], m_half[:], ALU.pow).then_inc(g_rs3, 1)
            if live(i):
                pool.wait_ge(v_ln2, 3 * (i + 1))
                pool.tensor_tensor(rs2[:, 1:2], rs2[:, 0:1], m_half[:], ALU.pow).then_inc(g_rs2, 1)
            if live(c):
                pool.wait_ge(v_n3, c + 1)
                pool.tensor_tensor(x_tile(c), x_tile(c), b_base[:], ALU.add).then_inc(g_xb, 1)
            if live(b):
                pool.wait_ge(v_qkv, b + 1)
                wait(pool, v_att, 3 * b)
                score_product(pool, D_VE, DH).then_inc(g_m1, 1)
            if live(i) and not (isinstance(i, int) and i == NC - 1):
                h_rest(i + 1)

        pool.wait_ge(c_pool, 1)
        pool.wait_ge(w_in[2], 64)
        pipeline(step)

    @block.scalar
    def _(act):
        def h_round(c):
            wait(act, s_a, c)
            act.activation(h_hi[:], h[:, :, bass.ds(c * P, P)], ACT.Copy).then_inc(a_h, 1)

        h_round(0)
        for n, (hi, lo, raw) in enumerate(weights()):
            if n == 0:
                act.wait_ge(w_sum, 1)
            if n == 1:
                act.wait_ge(w_in[1], 16)
            if n == 2:
                act.wait_ge(w_in[3], 32)
            if n == 4:
                act.wait_ge(w_wb, 16)
            act.activation(hi, raw, ACT.Copy).then_inc(w_hi_s, 1)

        def step(i):
            b, c, d = i - 1, i - 2, i - 3
            if live(b):
                act.wait_ge(s_t2, b + 1)
                wait(act, s_b, b)
                act.activation(flat(n2_hi[:]), p_t2[:], ACT.Copy).then_inc(a_n2, 1)
            if live(d):
                act.wait_ge(s_t4, d + 1)
                wait(act, s_dl, d)
                act.activation(hw_hi[:], p_t4[:, 0:P], ACT.Copy).then_inc(a_hw, 1)
            if live(c):
                act.wait_ge(s_t3, c + 1)
                wait(act, s_c, c)
                act.activation(flat(n3_hi[:]), p_t3[:], ACT.Copy).then_inc(a_n3, 1)
            if live(i) and not (isinstance(i, int) and i == NC - 1):
                h_round(i + 1)
            if live(b):
                act.wait_ge(v_den, 4 * b + 3)
                act.activation(flat(s[:]), flat(s[:]), ACT.Exp, scale=1.0 / float(np.sqrt(DH))).then_inc(a_exp, 1)
            if live(c):
                act.wait_ge(v_rt, 8 * c + 2)
                act.activation(rt[:, 0:1], m8[:, 0:1], ACT.Exp, scale=-1.0, bias=m8[:, 1:2]).then_inc(a_rt, 1)

        pipeline(step)

    @block.vector
    def _(ve):
        ve.wait_ge(w_in[0], 16)
        ve.tensor_reduce(flat(wq_sum[:]), prod[:].rearrange("p (n r) -> p n r", r=REP), AX.X, ALU.add).then_inc(w_sum, 1)
        ve.wait_ge(w_in[2], 64)
        ve.tensor_reduce(b_qkv[:, 0:QW], bq_raw[:].rearrange("p (n r) -> p n r", r=REP), AX.X, ALU.add)\
            .then_inc(w_sum, 1)

        def layer_stats(x, st, mv, rs, count, c):
            ve.bn_stats(st[:], x).then_inc(count, 1)
            ve.wait_ge(count, 3 * c + 1)
            ve.bn_aggr(mv[:], st[:]).then_inc(count, 1)
            ve.wait_ge(count, 3 * c + 2)
            ve.tensor_scalar(rs[:, 0:1], mv[:, 1:2], EPS, None, ALU.add).then_inc(count, 1)

        def step(i):
            b, c, d = i - 1, i - 2, i - 3
            if live(b):
                ve.wait_ge(a_n2, b + 1)
                ve.tensor_tensor(flat(n2_lo[:]), p_t2[:], flat(n2_hi[:]).bitcast(F32), ALU.subtract).then_inc(v_lo2, 1)
            if live(d):
                ve.wait_ge(a_hw, d + 1)
                ve.tensor_tensor(hw_lo[:], p_t4[:, 0:P], hw_hi[:].bitcast(F32), ALU.subtract).then_inc(v_lo4, 1)
            if live(c):
                ve.wait_ge(a_exp, c + 1)
                ve.tensor_reduce(den[:], s[:], AX.X, ALU.add).then_inc(v_den, 1)
                value_product(ve, 0, D_VE).then_inc(v_att, 1)
                ve.wait_ge(v_den, 4 * (c + 1))
                ve.reciprocal(den[:], den[:]).then_inc(v_att, 1)
                ve.wait_ge(v_att, 3 * c + 2)
                ve.wait_ge(g_m2, c + 1)
                ve.tensor_reduce(flat(o[:]), prod[:].rearrange("p (n e) -> p n e", e=DH), AX.X, ALU.add)\
                    .then_inc(v_att, 1)
                ve.wait_ge(v_att, 3 * (c + 1))
                ve.tensor_tensor(o[:], o[:], den[:].unsqueeze(2).broadcast_to([P, DH, HK]), ALU.mult).then_inc(v_x3, 1)
                ve.wait_ge(v_x3, 2 * c + 1)
                x = x_tile(c).rearrange("p (n r) -> p n r", r=REP)
                ve.tensor_tensor(x, x, flat(o[:]).unsqueeze(2).broadcast_to([P, QW, REP]), ALU.add).then_inc(v_x3, 1)
                ve.wait_ge(v_x3, 2 * (c + 1))
                layer_stats(x_tile(c), st3, mv3, rs3, v_ln3, c)
            if live(i):
                ve.wait_ge(s_a, i + 1)
                ve.tensor_tensor(x_tile(i), x_tile(i), p_a[:], ALU.add).then_inc(v_add, 1)
                ve.wait_ge(v_add, i + 1)
                layer_stats(x_tile(i), st2, mv2, rs2, v_ln2, i)
            if live(c):
                ve.wait_ge(g_rs3, c + 1)
                wait(ve, s_t3, c)
                ve.tensor_scalar(rows3[:], x_tile(c), mv3[:, 0:1], rs3[:, 1:2], ALU.subtract, ALU.mult).then_inc(v_n3, 1)
            if live(i):
                ve.wait_ge(g_rs2, i + 1)
                wait(ve, s_t2, i)
                ve.tensor_scalar(rows2[:], x_tile(i), mv2[:, 0:1], rs2[:, 1:2], ALU.subtract, ALU.mult).then_inc(v_n2, 1)
            if live(c):
                ve.wait_ge(a_n3, c + 1)
                ve.tensor_tensor(flat(n3_lo[:]), p_t3[:], flat(n3_hi[:]).bitcast(F32), ALU.subtract).then_inc(v_lo3, 1)
            if live(d):
                ve.wait_ge(s_dl, d + 1)
                ve.wait_ge(g_xb, d + 1)
                wait(ve, s_store, 16 * d)
                ve.tensor_tensor(out_t[:], x_tile(d), p_c[:], ALU.add).then_inc(v_fin, 1)
            if live(b):
                ve.wait_ge(s_b, b + 1)
                wait(ve, v_att, 3 * b)
                ve.tensor_tensor(qkv[:], p_b[:, 0:QKV], b_qkv[:], ALU.add).then_inc(v_qkv, 1)
                ve.wait_ge(v_qkv, b + 1)
                score_product(ve, 0, D_VE).then_inc(v_m1, 1)
                ve.wait_ge(v_m1, b + 1)
                ve.wait_ge(g_m1, b + 1)
                ve.tensor_reduce(flat(s[:]), prod[:].rearrange("p (n h) -> p n h", h=HK), AX.X, ALU.add).then_inc(v_den, 1)
                ve.wait_ge(v_den, 4 * b + 1)
                ve.tensor_reduce(mx[:], s[:], AX.X, ALU.max).then_inc(v_den, 1)
                ve.wait_ge(v_den, 4 * b + 2)
                ve.tensor_tensor(s[:], s[:], mx[:].unsqueeze(2).broadcast_to([P, DH, DH]), ALU.subtract)\
                    .then_inc(v_den, 1)
            if live(c):
                k = 8 * c
                ve.wait_ge(s_c, c + 1)
                ve.tensor_copy(lg[:], p_r[:, ER:ER + E]).then_inc(v_rt, 1)
                ve.wait_ge(v_rt, k + 1)
                ve.max(m8[:], lg[:]).then_inc(v_rt, 1)
                ve.wait_ge(v_rt, k + 2)
                ve.max_index(i8[:], m8[:], lg[:]).then_inc(v_rt, 1)
                ve.wait_ge(v_rt, k + 3)
                ve.tensor_copy(sel[:], i8[:, 0:2]).then_inc(v_rt, 1)
                ve.wait_ge(a_rt, c + 1)
                ve.tensor_scalar(rt[:, 1:2], rt[:, 0:1], 1.0, None, ALU.add).then_inc(v_rt, 1)
                ve.wait_ge(v_rt, k + 5)
                ve.reciprocal(rt[:, 2:3], rt[:, 1:2]).then_inc(v_rt, 1)
                ve.tensor_scalar(w8b[:], expert[:], sel[:, 1:2], rt[:, 0:1], ALU.is_equal, ALU.mult).then_inc(v_rt, 1)
                ve.wait_ge(v_rt, k + 7)
                ve.scalar_tensor_tensor(out=w8[:], in0=expert[:], scalar=sel[:, 0:1], in1=w8b[:],
                                        op0=ALU.is_equal, op1=ALU.add).then_inc(v_rt, 1)
                ve.wait_ge(v_rt, k + 8)
                ve.tensor_scalar(w8b[:], w8[:], rt[:, 2:3], LORA_SCALE, ALU.mult, ALU.mult).then_inc(v_hw, 1)
                ve.wait_ge(v_hw, 2 * c + 1)
                ve.tensor_tensor(hw[:].rearrange("p (e r) -> p e r", e=E), p_r[:, 0:ER].rearrange("p (e r) -> p e r", e=E),
                                 w8b[:].unsqueeze(2).broadcast_to([P, E, RANK]), ALU.mult).then_inc(v_hw, 1)

        pipeline(step)

    @block.tensor
    def _(pe):
        def step(i):
            b, c, d = i - 1, i - 2, i - 3
            if live(b):
                pe.wait_ge(v_n2, b + 1)
                wait(pe, v_lo2, b)
                for k in range(KT):
                    mm = pe.transpose(p_t2[:, k * P:(k + 1) * P], rows2[:, k * P:(k + 1) * P], ident[:])
                mm.then_inc(s_t2, 1)
            if live(d):
                pe.wait_ge(v_hw, 2 * (d + 1))
                wait(pe, v_lo4, d)
                pe.transpose(p_t4[:, 0:P], hw[:], ident[:]).then_inc(s_t4, 1)
            if live(i):
                pe.wait_ge(g_h, i + 1)
                wait(pe, v_add, i)
                three_pass(pe, p_a[:], lambda k: (h_hi[:, k, :], h_lo[:, k, :]),
                           lambda k: (wd_hi[:, k, :], wd_lo[:, k, :]), NT).then_inc(s_a, 1)
            if live(c):
                pe.wait_ge(v_n3, c + 1)
                wait(pe, v_lo3, c)
                for k in range(KT):
                    mm = pe.transpose(p_t3[:, k * P:(k + 1) * P], rows3[:, k * P:(k + 1) * P], ident[:])
                mm.then_inc(s_t3, 1)
            if live(d):
                pe.wait_ge(v_lo4, d + 1)
                for n, (x, w) in enumerate(((hw_hi, wl_hi), (hw_hi, wl_lo), (hw_lo, wl_hi))):
                    mm = pe.matmul(p_c[:], x[:], w[:], start=False, stop=(n == 2))
                mm.then_inc(s_dl, 1)
            if live(b):
                pe.wait_ge(v_lo2, b + 1)
                wait(pe, v_qkv, b)
                if isinstance(b, int) and b == 0:
                    pe.wait_ge(w_lo_s, 2)
                three_pass(pe, p_b[:, 0:QKV], lambda k: (n2_hi[:, k, :], n2_lo[:, k, :]),
                           lambda k: (qkv_hi[:, k, :], qkv_lo[:, k, :]), KT).then_inc(s_b, 1)
            if live(c):
                pe.wait_ge(v_lo3, c + 1)
                wait(pe, v_fin, c)
                wait(pe, v_hw, 2 * c)
                if isinstance(c, int) and c == 0:
                    pe.wait_ge(w_lo_s, 5)
                three_pass(pe, p_r[:, 0:ER + E], lambda k: (n3_hi[:, k, :], n3_lo[:, k, :]),
                           lambda k: (wa_hi[:, k, :], wa_lo[:, k, :]), KT)
                for k in range(KT):
                    for n, (x, w) in enumerate(((n3_hi, wb_hi), (n3_hi, wb_lo), (n3_lo, wb_hi))):
                        mm = pe.matmul(p_c[:], x[:, k, :], w[:, k, :], start=(k == 0 and n == 0), stop=False)
                mm.then_inc(s_c, 1)

        pipeline(step)


def program(nc, io, stages=4):
    with ExitStack() as outer:
        def sb(ctx, name, shape, dt=F32):
            return ctx.enter_context(nc.sbuf_tensor(name, shape, dt))
        x_res = sb(outer, "x_res", [P, NC, D])
        ident = sb(outer, "identity", [P, P])
        with ExitStack() as ctx:
            mixer(nc, io, ctx, x_res, ident)
        with ExitStack() as held:
            h = sb(held, "h", [P, NT, L])
            wd_hi = sb(held, "wd_hi", [P, NT, D], F32R)
            wd_lo = sb(held, "wd_lo", [P, NT, D], F32R)
            with ExitStack() as ctx:
                swiglu_up(nc, io, ctx, x_res, h, wd_hi, wd_lo, ident)
            with ExitStack() as ctx:
                token_tiles(nc, io, ctx, x_res, h, wd_hi, wd_lo, ident)


def layouts(v):
    f = {k: np.ascontiguousarray(np.asarray(a)) for k, a in v.items()}
    io = {"x": f["L0_attn_hidden_states"].reshape(L, D)}
    wi = f["L0_attn_in_proj_w"]
    inner = H * HD
    gate, x, b, c, dt = np.split(wi, np.cumsum([inner, inner, G * NS, G * NS]), axis=0)

    def conv_rows(a):
        a, ab, ac = a
        return np.concatenate([a.reshape((G, GW // P, P) + a.shape[1:]), ab.reshape((G, 1, P) + a.shape[1:]),
                               ac.reshape((G, 1, P) + a.shape[1:])], axis=1)
    cw = conv_rows((x, b, c)).reshape(G, TILES, P, KT, P).transpose(0, 1, 4, 3, 2).reshape(G, TILES, P, 512)
    gw = gate.reshape(G, GW, KT, P).transpose(0, 2, 3, 1)
    ow = f["L0_attn_out_proj_w"].reshape(D, G, GW // P, P).transpose(1, 2, 3, 0)
    io["w"] = np.concatenate([cw, gw, ow], axis=1).reshape(G * WT, P, 512)
    dt2 = np.concatenate([dt, dt], axis=0)
    io["w_dt"] = dt2.reshape(P, KT, P).transpose(2, 1, 0).reshape(P, 512)
    kw = np.concatenate([f["L0_attn_conv_weight"], f["L0_attn_conv_bias"][:, None]], axis=1)
    io["conv_w"] = conv_rows(np.split(kw, [inner, inner + G * NS])).transpose(2, 0, 1, 3)
    io["norm_w"] = f["L0_attn_norm_weight"].reshape(G, GW // P, P).transpose(2, 0, 1)
    hc = np.stack([f["L0_attn_dt_bias"], f["L0_attn_A_log"]], axis=1)
    io["head_c"] = np.concatenate([hc, hc], axis=0)
    io["d"] = f["L0_attn_D"].reshape(1, H)
    io["ident"] = np.eye(P, dtype=np.float32)
    io["tri"] = np.triu(np.ones((P, P), np.float32))
    t = np.arange(P)
    thr = 2 * np.arange(1, NTHR + 1)
    lhs = np.zeros((KD, P), np.float32)
    lhs[:PART] = 1
    lhs[PART + PART * HG:] = t[None] >= thr[:, None]
    rhs = np.zeros((KD, HG, P), np.float32)
    for k in range(PART):
        for h in range(HG):
            rhs[PART + k * HG + h, h] = -1
    rhs[PART + PART * HG:] = MASK * (t[None] < thr[:, None])[:, None, :]
    io["d_lhs"] = lhs.astype(np.dtype("bfloat16"))
    io["d_rhs"] = rhs.reshape(KD, HG * P).astype(np.dtype("bfloat16"))

    def pad(a, n, axis):
        w = [(0, 0)] * a.ndim
        w[axis] = (0, n - a.shape[axis])
        return np.pad(a, w)
    gu = [np.repeat(pad(f[f"L0_ffn_{m}_qweight"], NI, 1), 8, axis=0).reshape(KT, P, NT, P).transpose(2, 1, 0, 3)
          .reshape(NT, P, 512) for m in ("gate", "up")]
    dn = np.repeat(pad(f["L0_ffn_down_qweight"], NI // 8, 0), 8, axis=0).reshape(NT, P, D)
    io["q"] = np.stack([gu[0], gu[1], dn], axis=1).reshape(3 * NT, P, 512)
    io["sc_gu"] = np.concatenate([pad(f[f"L0_ffn_{m}_scales"], NI, 1) for m in ("gate", "up")], axis=1).reshape(P, -1)
    io["sc_d"] = f["L0_ffn_down_scales"].reshape(P, -1)
    io["zq_gu"] = np.concatenate([pad(f[f"L0_ffn_{m}_qzeros"], NI // 8, 1) for m in ("gate", "up")], axis=1)
    io["zq_d"] = f["L0_ffn_down_qzeros"]
    io["gi_gu"] = np.concatenate([f["L0_ffn_gate_g_idx"], f["L0_ffn_up_g_idx"]]).reshape(1, -1)
    io["gi_d"] = pad(f["L0_ffn_down_g_idx"], NI, 0).reshape(1, -1)
    io["shift"] = (4 * (np.arange(P) % 8)).astype(np.int32).reshape(P, 1)
    n = np.arange(PART * GD)
    io["row_of"] = np.stack([n % GU, n % GD], axis=1).astype(np.float32)

    def by_row(a):
        return a.reshape(KT, P, -1).transpose(1, 0, 2).reshape(P, -1)
    io["wq"] = by_row(f["L1_attn_Wq"])
    io["wkv"] = by_row(np.concatenate([f["L1_attn_Wk"].reshape(D, -1), f["L1_attn_Wv"].reshape(D, -1)], axis=1))
    io["bq"] = f["L1_attn_bq"].reshape(1, -1)
    io["bkv"] = np.concatenate([f["L1_attn_bk"].reshape(-1), f["L1_attn_bv"].reshape(-1)]).reshape(1, -1)
    io["wb"] = by_row(f["L1_ffn_W_base"].T)
    io["b_base"] = f["L1_ffn_b_base"].reshape(1, -1)
    io["wa"] = by_row(np.concatenate([f["L1_ffn_A"].reshape(ER, D), f["L1_ffn_W_router"]], axis=0).T)
    io["wl"] = f["L1_ffn_B"].transpose(0, 2, 1).reshape(ER, D)
    io["expert"] = np.arange(E, dtype=np.float32).reshape(1, E)
    return {k: np.ascontiguousarray(a) for k, a in io.items()}


def kernel(**inputs):
    import concourse.bacc as bacc
    from concourse.bass_utils import run_bass_kernel_spmd

    arrays = layouts(inputs)
    nc = bacc.Bacc("TRN2", target_bir_lowering=False, num_devices=1)
    io = {k: nc.dram_tensor(k, a.shape, mybir.dt.from_np(a.dtype), kind="ExternalInput").ap()
          for k, a in arrays.items()}
    io["out"] = nc.dram_tensor("out", (L, D), F32, kind="ExternalOutput").ap()
    program(nc, io)
    r = run_bass_kernel_spmd(nc, [arrays], core_ids=[0])
    return r.results[0]["out"].reshape(1, L, D)
```

```python
from contextlib import ExitStack

import numpy as np

import concourse.bass as bass
from concourse import mybir

F32 = mybir.dt.float32
F32R = mybir.dt.float32r
BF16 = mybir.dt.bfloat16
I32 = mybir.dt.int32
U32 = mybir.dt.uint32
ALU = mybir.AluOpType
ACT = mybir.ActivationFunctionType
AX = mybir.AxisListType

P = 128
L = 1024
D = 512
KT = D // P
HALF = L // 2
NC = L // P
CH = NC // 2

H = 64
HD = 64
G = 8
HG = H // G
GW = HG * HD
NS = 128
TAPS = 4
TILES = GW // P + 2
TB, TC = TILES - 2, TILES - 1
WT = TILES + KT + GW // P
RAW = 4
EPS = 1e-5
LOG_FLOOR = -87.0
PART = 3
NTHR = 63
KD = PART + PART * HG + NTHR
MASK = -32768.0


INTER = 1376
GRP = 128
NT = -(-INTER // P)
GU = D // GRP
GD = INTER // GRP
NI = NT * P
NSC = 2 * GU * NI // P
NSD = GD * D // P
NGI = 2 * D // P
NGD = NI // P


def wait(eng, sem, count):
    if isinstance(count, int) and count <= 0:
        return
    eng.wait_ge(sem, count)


def at(eng, value):
    return value if isinstance(value, int) else eng.snap(value)


def three_pass(pe, out, lhs, rhs, k_tiles):
    last = None
    for k in range(k_tiles):
        (lh, ll), (rh, rl) = lhs(k), rhs(k)
        for n, (a, b) in enumerate(((lh, rh), (lh, rl), (ll, rh))):
            last = pe.matmul(out, a, b, start=(k == 0 and n == 0), stop=(k == k_tiles - 1 and n == 2))
    return last


def mixer(nc, io, ctx, x_res, ident, mean_var2, rstd2, q_prep):
    def sb(name, shape, dt=F32):
        return ctx.enter_context(nc.sbuf_tensor(name, shape, dt))

    def pb(name):
        return ctx.enter_context(nc.psum_tensor(name, [P, 512], F32))

    def sem(name):
        return ctx.enter_context(nc.semaphore(name))

    xn_hi = sb("xn_hi", [P, KT, L], F32R)
    xn_lo = sb("xn_lo", [P, KT, L], F32R)
    w_raw = sb("w_raw", [P, RAW, 512])
    w_hi = sb("w_hi", [P, WT, 512], F32R)
    w_lo = sb("w_lo", [P, WT, 512], F32R)
    conv_w = sb("conv_taps", [P, G, TILES, TAPS + 1])
    norm_w = sb("norm_scale", [P, G, GW // P])
    pre = sb("pre", [P, 2, HALF + TAPS - 1])
    halo = sb("halo", [P, TILES, TAPS - 1])
    conv = sb("conv", [P, 2, HALF])
    conv_th = sb("conv_th", [P, 2, HALF])
    xbc = sb("xbc", [P, TILES, L])
    d_lhs = sb("decay_lhs", [KD, 2, P], BF16)
    d_rhs = sb("decay_rhs", [KD, 2, HG * P], BF16)
    em = sb("em", [P, 2, HG * P])
    gm = sb("gm", [P, P])
    b_tok = sb("b_tok", [P, P])
    xs = sb("xs", [P, 2, GW])
    x_dt = sb("x_dt", [P, GW])
    x_w = sb("x_w", [P, GW])
    x_d = sb("x_d", [P, GW])
    y = sb("y", [P, 2, GW])
    gate_th = sb("gate_th", [P, GW])
    gate = sb("gate", [P, GW])
    z = sb("z", [P, GW])
    zt_hi = sb("zt_hi", [P, GW // P, P], F32R)
    zt_lo = sb("zt_lo", [P, GW // P, P], F32R)
    junk = sb("junk", [P, GW])
    state = sb("state", [P, GW])
    state_dec = sb("state_dec", [P, GW])
    dt_t = sb("dt_t", [P, NC, H])
    dtw_t = sb("dtw_t", [P, NC, H])
    ecum_t = sb("ecum_t", [P, NC, H])
    etot_t = sb("etot_t", [P, NC, H])
    head_g = sb("head_g", [P, 4, NC, HG])
    d_g = sb("d_g", [P, HG])
    tri = sb("tri_mask", [P, P])
    d_b = sb("d_b", [P, H])
    head_c = sb("head_consts", [P, 4])
    stats = sb("stats", [P, NC, 6])
    mean_var = sb("mean_var", [P, NC, 2])
    rstd = sb("rstd", [P, NC])
    m_half = sb("m_half", [P, 1])
    ss = sb("ss", [P, 2])
    ssv = sb("ssv", [P, 2])
    g_rstd = sb("g_rstd", [P, 2])
    xnt = xs

    p_tile, p_gate, p_d0, p_d1 = pb("p_tile"), pb("p_gate"), pb("p_d0"), pb("p_d1")
    p_x, p_in, p_y, p_gb = pb("p_x"), pb("p_in"), pb("p_y"), pb("p_gb")

    parts = nc.dram_tensor("cum_parts", [G, PART, HG, L], BF16, kind="Internal").ap()
    w_rows = io["w"].rearrange("n p c -> (n p) c")

    s_x = [sem(f"s_x{i}") for i in range(NC)]
    s_const = sem("s_const")
    s_halved = sem("s_halved")
    s_raw = [sem(f"s_raw{i}") for i in range(RAW)]
    s_dl = [sem("s_dl0"), sem("s_dl1")]
    s_parts = sem("s_parts")
    s_dconst = sem("s_dconst")
    ln_st, ln_var, ln_rs, ln_xn, ln_tr, ln_hi, ln_lo = (sem(f"ln_{k}") for k in "abcdefg")
    dt_mm, dt_ve, dt_ac, dt_tp = (sem(f"dt_{k}") for k in ("mm", "ve", "ac", "tp"))
    s_split_dt = sem("s_split_dt")
    s_q_in, s_q_ve, s_q_out = sem("s_q_in"), sem("s_q_ve"), sem("s_q_out")
    l2_st, l2_var, l2_rs = (sem(f"l2_{k}") for k in ("st", "var", "rs"))
    s_xt, s_gb, s_d, s_prj, s_gate, s_zt, s_out, s_inter, s_intra, s_stn = (
        sem(f"pe_{k}") for k in ("xt", "gb", "d", "prj", "gate", "zt", "out", "inter", "intra", "stn"))
    s_xs, s_e, s_cin, s_th, s_tg, s_zhi, s_ss, s_whi = (
        sem(f"act_{k}") for k in ("xs", "e", "cin", "th", "tg", "zhi", "ss", "whi"))
    s_head = sem("ve_head")
    s_gm, s_m, s_halo, s_tap, s_xc, s_sg, s_zlo, s_res, s_t, s_y, s_z, s_stu, s_v, s_wloo = (
        sem(f"ve_{k}") for k in ("gm", "m", "halo", "tap", "xc", "sg", "zlo", "res", "t", "y", "z",
                                 "stu", "v", "wloo"))
    s_xdt, s_xw, s_xd, s_std, s_txd, s_rs, s_wlo = (
        sem(f"pool_{k}") for k in ("xdt", "xw", "xd", "std", "txd", "rs", "wlo"))

    MADE_IN = [(0, 1), (2, 3), (4,), (5,)]
    SPLIT_IN = {1: (0, 1), 2: (2, 3), 3: (4,), 4: (5,), 7: (6, 7, 8, 9)}
    LAST = NC * G - 1

    VE_LO = [TILES, TILES + 1] + list(range(TILES + KT, WT))
    POOL_LO = [w for w in range(WT) if w not in VE_LO]

    def lo_count(g, w):
        if w < 0:
            g, w = g - 1, w + WT
        tiles, s = (VE_LO, s_wloo) if w in VE_LO else (POOL_LO, s_wlo)
        return s, g * len(tiles) + tiles.index(w) + 1

    def half_cols(hf):
        return slice(hf * HALF, (hf + 1) * HALF)

    def conv_tiles(g, last, c):
        def made(c):
            if last and c >= CH:
                return []
            half = 2 * g + c // CH + 1
            return [(half * TILES + j, g + c // CH, j, 1 - c // CH) for j in MADE_IN[c % CH]]
        return (made(c - 1)[1:] if c % CH else []), made(c)

    def heads(k, c):
        return head_g[:, k, c, :].unsqueeze(2).broadcast_to([P, HG, HD])

    DT, DTW, ECUM, ETOT = range(4)

    def by_head(ap):
        return ap.rearrange("p (h d) -> p h d", h=HG)

    t_v, t_a, t_dt, t_r, t_rem = (xbc[:, j, HALF:L] for j in range(5))
    def by_half(a):
        return a[:].rearrange("p (a c) h -> p a c h", a=2)

    def transposed(p):
        return p[:].rearrange("p (c a h) -> p a c h", c=CH, a=2)

    t_e, t_cum = em[:, 0, 0:HALF], em[:, 1, 0:HALF]
    t_w = y[:, 0, :]
    t_parts = [x[:, 0:GW // 2].bitcast(BF16) for x in (x_dt, x_w, x_d)]
    t_mask = junk[:, 0:GW // 2].bitcast(BF16)

    q_raw, q_rest = conv[:, 0, 0:NSC + NSD], conv[:, 1, 0:NSC + NSD]
    q_parts = [conv_th[:, 0, k * GRP:k * GRP + (NSC + NSD) // 2].bitcast(BF16) for k in range(PART)]
    q_zero = pre[:, 0, 0:NSC + NSD].bitcast(I32)
    q_zero4 = pre[:, 0, GRP:GRP + NSC + NSD].bitcast(I32)
    q_zero1 = pre[:, 0, 2 * GRP:2 * GRP + (NSC + NSD) // 2].bitcast(BF16)
    q_index = pre[:, 1, 0:NGI + NGD].bitcast(I32)
    q_index_f = pre[:, 1, GRP:GRP + NGI + NGD]
    q_shift = pre[:, 1, 2 * GRP:2 * GRP + 1].bitcast(I32)

    block = ctx.enter_context(nc.Block())

    @block.sync
    def _(sp):
        for c in range(NC):
            sp.dma_start(x_res[:, c, :], io["x"][c * P:(c + 1) * P, :]).then_inc(s_x[c], 16)
            if c == 1:
                sp.dma_start(ident[:], io["ident"]).then_inc(s_const, 16)
                sp.dma_start(head_c[:, 0:2], io["head_c"]).then_inc(s_const, 16)
                sp.dma_start(z[:], io["w_dt"]).then_inc(s_const, 16)
        sp.dma_start(conv_w[:], io["conv_w"]).then_inc(s_const, 16)
        sp.dma_start(norm_w[:], io["norm_w"]).then_inc(s_const, 16)
        sp.dma_start(tri[:], io["tri"]).then_inc(s_const, 16)
        sp.dma_start(d_b[:], io["d"].broadcast_to([P, H])).then_inc(s_const, 16)
        for i in range(2):
            sp.dma_start(d_lhs[:, i, :], io["d_lhs"]).then_inc(s_dconst, 16)
            sp.dma_start(d_rhs[:, i, :], io["d_rhs"]).then_inc(s_dconst, 16)

        def load_w(g, w):
            row = at(sp, (g * WT + w) * P)
            before = w - RAW if w >= RAW else w + (WT - 1 - w) // RAW * RAW - WT
            split, count = lo_count(g, before)
            wait(sp, split, at(sp, count))
            sp.dma_start(w_raw[:, w % RAW, :], w_rows[bass.ds(row, P), :]).then_inc(s_raw[w % RAW], 16)

        def load_d(g, c):
            n = g * NC + c
            lhs_row, rhs_row = at(sp, g * PART * HG), at(sp, g * PART)
            wait(sp, s_d, n - 1)
            cs = slice(c * P, (c + 1) * P)
            sp.dma_start(d_lhs[PART:PART + PART * HG, c % 2, :],
                         parts.rearrange("g k h t -> (g k h) t")[bass.ds(lhs_row, PART * HG), cs])\
                .then_inc(s_dl[c % 2], 16)
            sp.dma_start(d_rhs[0:PART, c % 2, :].rearrange("k (h t) -> k h t", h=HG),
                         parts.rearrange("g k h t -> (g k) h t")[bass.ds(rhs_row, PART), :, cs])\
                .then_inc(s_dl[c % 2], 16)

        for w in range(TILES + KT):
            load_w(0, w)
        for k in range(PART):
            wait(sp, dt_ve, 13 + k)
            for a in range(2):
                sp.dma_start(parts[:, k, :, a * HALF:(a + 1) * HALF], t_parts[k][a * H:(a + 1) * H, :])\
                    .then_inc(s_parts, 16)
        sp.wait_ge(s_parts, 16 * PART * 2)
        sp.wait_ge(s_dconst, 64)
        load_d(0, 0)
        load_d(0, 1)

        def group(g, last):
            for c in range(NC):
                if c + 2 < NC:
                    load_d(g, c + 2)
                elif not last:
                    load_d(g + 1, c + 2 - NC)
                if not last:
                    for w in {0: (0, 1, 2, 3), 1: (4, 5), 2: (6, 7), 4: (8, 9)}.get(c, ()):
                        load_w(g + 1, w)
                if last and c == CH:
                    sp.wait_ge(s_xc, 2 * G * TILES)
                    sp.wait_ge(s_tap, 2 * G * TILES * TAPS)
                    for dst, k in ((q_raw, "q_scales"), (q_zero, "q_zeros"), (q_index, "q_index"), (q_shift, "z_shift")):
                        sp.dma_start(dst, io[k]).then_inc(s_q_in, 16)

        def out_weights(g):
            for w in range(TILES + KT, WT):
                load_w(g, w)

        out_weights(0)
        group(0, False)
        with sp.Fori(1, G - 1) as g:
            out_weights(g)
            group(g, False)
        out_weights(G - 1)
        group(G - 1, True)
        sp.wait_ge(s_q_ve, 12)
        for k in range(PART):
            sp.dma_start(q_prep["sc_gu"][k], q_parts[k][:, 0:NSC]).then_inc(s_q_out, 16)
            sp.dma_start(q_prep["sc_d"][k], q_parts[k][:, NSC:]).then_inc(s_q_out, 16)
        sp.dma_start(q_prep["zp_gu"], q_zero1[:, 0:NSC]).then_inc(s_q_out, 16)
        sp.dma_start(q_prep["zp_d"], q_zero1[:, NSC:]).then_inc(s_q_out, 16)
        sp.dma_start(q_prep["gi_gu"], q_index_f[:, 0:NGI]).then_inc(s_q_out, 16)
        sp.dma_start(q_prep["gi_d"], q_index_f[:, NGI:]).then_inc(s_q_out, 16)
        sp.wait_ge(s_q_out, 16 * (2 * PART + 4))

    @block.gpsimd
    def _(pool):
        def group(g, last):
            for c in range(NC):
                n = g * NC + c
                st = g * (NC - 1) + c
                if c > 0:
                    pool.wait_ge(s_stu, n)
                    pool.tensor_tensor(by_head(state_dec[:]), by_head(state[:]), heads(ETOT, c), ALU.mult)\
                        .then_inc(s_std, 1)
                if c == 0:
                    pool.wait_ge(s_head, 5 * (g + 1))
                pool.wait_ge(s_xs, n + 1)
                wait(pool, s_stn, n)
                pool.tensor_tensor(by_head(x_w[:]), by_head(xs[:, c % 2, :]), heads(DTW, c), ALU.mult)\
                    .then_inc(s_xw, 1)
                wait(pool, s_intra, n)
                pool.tensor_tensor(by_head(x_dt[:]), by_head(xs[:, c % 2, :]), heads(DT, c), ALU.mult)\
                    .then_inc(s_xdt, 1)
                if not (isinstance(g, int) and n == 0):
                    norm(n - 1, (c - 1) % 2)
                wait(pool, s_y, n)
                pool.tensor_tensor(by_head(x_d[:]), by_head(xs[:, c % 2, :]),
                                   d_g[:].unsqueeze(2).broadcast_to([P, HG, HD]), ALU.mult)\
                    .then_inc(s_xd, 1)
                splits = () if last else SPLIT_IN.get(c, ())
                for w in splits:
                    if w in POOL_LO:
                        w_rest(g + 1, w)
                if c > 0:
                    pool.wait_ge(s_t, st)
                    pool.wait_ge(s_xd, n + 1)
                    pool.tensor_tensor(y[:, c % 2, :], y[:, c % 2, :], x_d[:], ALU.add).then_inc(s_txd, 1)
        def rstd_of(chunks, count):
            n = chunks.stop - chunks.start
            pool.wait_ge(l2_var, count)
            pool.tensor_tensor(rstd2[:, chunks], rstd2[:, chunks], m_half[:].broadcast_to([P, n]), ALU.pow)\
                .then_inc(l2_rs, 1)

        def norm(m, slot):
            pool.wait_ge(s_v, m + 1)
            pool.tensor_tensor(g_rstd[:, slot:slot + 1], ssv[:, slot:slot + 1], m_half[:], ALU.pow).then_inc(s_rs, 1)

        def w_rest(g, w):
            n = g * WT + w
            pool.wait_ge(s_whi, n + 1)
            pool.tensor_tensor(w_lo[:, w, :], w_raw[:, w % RAW, :], w_hi[:, w, :].bitcast(F32), ALU.subtract)\
                .then_inc(s_wlo, 1)

        pool.memset(m_half[:], -0.5).then_inc(ln_rs, 1)
        pool.wait_ge(ln_rs, 1)
        for c in range(NC):
            pool.wait_ge(ln_var, 2 * (c + 1))
            pool.tensor_tensor(rstd[:, c:c + 1], rstd[:, c:c + 1], m_half[:], ALU.pow).then_inc(ln_rs, 1)
        for w in POOL_LO:
            w_rest(0, w)
        pool.wait_ge(s_parts, 16 * PART * 2)
        group(0, False)
        with pool.Fori(1, G - 1) as g:
            group(g, False)
        group(G - 1, True)
        rstd_of(slice(0, NC - 1), NC)
        norm(LAST, (NC - 1) % 2)
        rstd_of(slice(NC - 1, NC), NC + 2)

    @block.scalar
    def _(act):
        def w_round(g, w):
            n = g * WT + w
            act.wait_ge(s_raw[w % RAW], 16 * (g * len(range(w % RAW, WT, RAW)) + w // RAW + 1))
            if w < TILES + KT:
                act.activation(w_hi[:, w, :], w_raw[:, w % RAW, :], ACT.Copy).then_inc(s_whi, 1)
            else:
                k = w - TILES - KT
                act.activation(w_hi[:, w, :], w_raw[:, w % RAW, :], ACT.Copy, scale=norm_w[:, bass.ds(g, 1), k])\
                    .then_inc(s_whi, 1)

        def tile_in(T, g, j, bank=0):
            p = (p_tile, p_d1)[bank]
            s = j % 2
            act.wait_ge(s_prj, T + 1)
            wait(act, s_xc, T - 1)
            act.activation(pre[:, s, TAPS - 1:], p[:], ACT.Copy).then_inc(s_cin, 1)
            act.activation(conv[:, s, :], p[:], ACT.Identity, bias=conv_w[:, bass.ds(g, 1), j, TAPS],
                           scale=conv_w[:, bass.ds(g, 1), j, TAPS - 1]).then_inc(s_cin, 1)

        def tile_tanh(T, j):
            act.wait_ge(s_tap, TAPS * (T + 1))
            act.activation(conv_th[:, j % 2, :], conv[:, j % 2, :], ACT.Tanh).then_inc(s_th, 1)

        def z_round(m):
            act.wait_ge(s_zt, m + 1)
            act.activation(zt_hi[:].rearrange("p k t -> p (k t)"), p_in[:], ACT.Copy).then_inc(s_zhi, 1)

        def gate_tanh(m):
            act.wait_ge(s_gate, m + 1)
            wait(act, s_sg, m)
            act.activation(gate_th[:], p_gate[:], ACT.Tanh, scale=0.5).then_inc(s_tg, 1)

        def group(g, last):
            for c in range(NC):
                n = g * NC + c
                first = isinstance(g, int) and n == 0
                left, made = conv_tiles(g, last, c)
                splits = () if last else SPLIT_IN.get(c, ())
                for T, tg, j, _ in left:
                    tile_in(T, tg, j)
                act.wait_ge(s_xt, n + 1)
                wait(act, s_xd, n - 1)
                act.activation(xs[:, c % 2, :], p_x[:], ACT.Copy).then_inc(s_xs, 1)
                if not first:
                    z_round(n - 1)
                act.wait_ge(s_d, n + 1)
                wait(act, s_intra, n - 1)
                for k, p in enumerate((p_d0, p_d1)):
                    act.activation(em[:, c % 2, k * 512:(k + 1) * 512], p[:], ACT.Exp).then_inc(s_e, 1)
                for T, tg, j, _ in left:
                    tile_tanh(T, j)
                if c == NC - 1 and not last:
                    act.wait_ge(s_gate, n + 1)
                for w in splits:
                    w_round(g + 1, w)
                for T, tg, j, _ in made[:1]:
                    tile_in(T, tg, j)
                    if not left:
                        tile_tanh(T, j)
                if c == 0:
                    wait(act, s_out, n)
                    w_round(g, TILES + KT)
                    w_round(g, TILES + KT + 1)
                act.wait_ge(s_y, n + 1)
                wait(act, s_ss, n)
                wait(act, s_v, n - 1)
                act.activation(junk[:], y[:, c % 2, :], ACT.Square, accum_out=ss[:, c % 2:c % 2 + 1])\
                    .then_inc(s_ss, 1)
                if left:
                    for T, tg, j, _ in made[:1]:
                        tile_tanh(T, j)
                if not (last and c == NC - 1):
                    gate_tanh(n + 1)
                if c == 0:
                    w_round(g, TILES + KT + 2)
                    w_round(g, TILES + KT + 3)

        for c in range(NC):
            act.wait_ge(ln_tr, c + 1)
            act.activation(xn_hi[:, :, c * P:(c + 1) * P], (p_x, p_in)[c % 2][:].rearrange("p (k t) -> p k t", k=KT),
                           ACT.Copy).then_inc(ln_hi, 1)
            if c >= CH:
                w_round(0, c - CH)
        act.wait_ge(s_halved, 2)
        act.wait_ge(dt_ve, 4)
        act.activation(t_e, t_v, ACT.Abs).then_inc(dt_ac, 1)
        act.wait_ge(dt_ac, 1)
        act.activation(t_e, t_e, ACT.Exp, scale=-1.0).then_inc(dt_ac, 1)
        act.activation(head_c[:, 3:4], head_c[:, 1:2], ACT.Exp).then_inc(dt_ac, 1)
        act.wait_ge(dt_ve, 5)
        act.activation(t_r, t_w, ACT.Ln).then_inc(dt_ac, 1)
        w_round(0, 4)
        w_round(0, 5)
        tile_in(0, 0, 0, 0)
        tile_in(1, 0, 1, 1)
        for w in range(TILES, TILES + KT):
            w_round(0, w)
        act.wait_ge(dt_tp, 4)
        act.activation(by_half(ecum_t), transposed(p_y), ACT.Exp).then_inc(dt_ac, 1)
        act.activation(by_half(dtw_t), transposed(p_gb), ACT.Exp).then_inc(dt_ac, 1)
        act.activation(by_half(etot_t), transposed(p_d0), ACT.Exp).then_inc(dt_ac, 1)
        for j in range(TILES):
            tile_tanh(j, j)
            if j + 2 < TILES:
                tile_in(j + 2, 0, j + 2, j % 2)
        gate_tanh(0)
        group(0, False)
        with act.Fori(1, G - 1) as g:
            group(g, False)
        group(G - 1, True)
        z_round(LAST)

    @block.vector
    def _(ve):
        def first_tap(T, g, j, hf):
            s = j % 2
            wait(ve, s_tap, TAPS * (T - 1))
            if hf == 0:
                ve.memset(pre[:, s, 0:TAPS - 1], 0.0).then_inc(s_halo, 1)
            else:
                ve.tensor_copy(pre[:, s, 0:TAPS - 1], halo[:, j, :]).then_inc(s_halo, 1)
            ve.wait_ge(s_cin, 2 * (T + 1))
            ve.wait_ge(s_halo, T + 1)
            tap(T, g, j, 0)

        def tap(T, g, j, k):
            s = j % 2
            wait(ve, s_tap, TAPS * T + k)
            ve.scalar_tensor_tensor(out=conv[:, s, :], in0=pre[:, s, k:k + HALF],
                                    scalar=conv_w[:, bass.ds(g, 1), j, k],
                                    in1=conv[:, s, :], op0=ALU.mult, op1=ALU.add).then_inc(s_tap, 1)

        def second_tap(T, g, j, hf):
            tap(T, g, j, 1)

        def last_tap(T, g, j, hf):
            tap(T, g, j, 2)
            ve.tensor_copy(halo[:, j, :], pre[:, j % 2, HALF:HALF + TAPS - 1]).then_inc(s_tap, 1)

        def silu(T, g, j, hf):
            ve.wait_ge(s_th, T + 1)
            ve.scalar_tensor_tensor(out=xbc[:, j, half_cols(hf)], in0=conv_th[:, j % 2, :], scalar=1.0,
                                    in1=conv[:, j % 2, :], op0=ALU.add, op1=ALU.mult).then_inc(s_xc, 1)

        def variance(m, slot):
            ve.wait_ge(s_ss, m + 1)
            wait(ve, s_rs, m - 1)
            ve.tensor_scalar(ssv[:, slot:slot + 1], ss[:, slot:slot + 1], 1.0 / GW, EPS, ALU.mult, ALU.add)\
                .then_inc(s_v, 1)

        def z_rest(m):
            ve.wait_ge(s_zhi, m + 1)
            ve.tensor_tensor(zt_lo[:].rearrange("p k t -> p (k t)"), p_in[:],
                             zt_hi[:].rearrange("p k t -> p (k t)").bitcast(F32), ALU.subtract).then_inc(s_zlo, 1)

        def residual(m, c):
            ve.wait_ge(s_out, m + 1)
            ve.wait_ge(s_rs, m + 1)
            wait(ve, s_res, m)
            ve.scalar_tensor_tensor(out=x_res[:, c, :], in0=p_y[:], scalar=g_rstd[:, c % 2:c % 2 + 1],
                                    in1=x_res[:, c, :], op0=ALU.mult, op1=ALU.add).then_inc(s_res, 1)

        def gate_silu(m):
            ve.wait_ge(s_tg, m + 1)
            wait(ve, s_z, m)
            ve.scalar_tensor_tensor(out=gate[:], in0=gate_th[:], scalar=1.0, in1=p_gate[:],
                                    op0=ALU.add, op1=ALU.mult).then_inc(s_sg, 1)

        def w_rest(g, w):
            ve.wait_ge(s_whi, g * WT + w + 1)
            raw, hi, lo = w_raw[:, w % RAW, :], w_hi[:, w, :].bitcast(F32), w_lo[:, w, :]
            if w < TILES + KT:
                ve.tensor_tensor(lo, raw, hi, ALU.subtract).then_inc(s_wloo, 1)
            else:
                ve.scalar_tensor_tensor(out=lo, in0=raw, scalar=norm_w[:, bass.ds(g, 1), w - TILES - KT],
                                        in1=hi, op0=ALU.mult, op1=ALU.subtract).then_inc(s_wloo, 1)

        def row_stats(g, k):
            ve.wait_ge(s_res, g * NC + k + 1)
            ve.bn_stats(stats[:, k, :], x_res[:, k, :]).then_inc(l2_st, 1)
            ve.wait_ge(l2_st, k + 1)
            ve.bn_aggr(mean_var2[:, k, :], stats[:, k, :]).then_inc(l2_var, 1)

        def variance_of(chunks):
            ve.wait_ge(l2_var, NC - 1 if chunks.stop < NC else NC + 1)
            ve.tensor_scalar(rstd2[:, chunks], mean_var2[:, chunks, 1], EPS, None, ALU.add).then_inc(l2_var, 1)

        def small_operands():
            ve.wait_ge(s_q_in, 16 * 4)
            ve.tensor_copy(q_parts[0], q_raw).then_inc(s_q_ve, 1)
            ve.tensor_scalar(q_zero4, q_zero, q_shift, 15, ALU.logical_shift_right, ALU.bitwise_and)\
                .then_inc(s_q_ve, 1)
            index = ((slice(0, NGI), GU), (slice(NGI, NGI + NGD), GD))
            for cols, groups in index:
                ve.tensor_scalar(q_index_f[:, cols], q_index[:, cols], 0.0, float(groups), ALU.is_lt, ALU.mult)\
                    .then_inc(s_q_ve, 1)
            ve.wait_ge(s_q_ve, 4)
            ve.tensor_tensor(q_rest, q_raw, q_parts[0], ALU.subtract).then_inc(s_q_ve, 1)
            ve.tensor_scalar(q_zero1, q_zero4, 1.0, None, ALU.add).then_inc(s_q_ve, 1)
            ve.tensor_tensor(q_index_f, q_index_f, q_index, ALU.add).then_inc(s_q_ve, 1)
            ve.wait_ge(s_q_ve, 7)
            ve.tensor_copy(q_parts[1], q_rest).then_inc(s_q_ve, 1)
            for cols, groups in index:
                ve.tensor_scalar(q_index_f[:, cols], q_index_f[:, cols], 0.0, float(groups - 1), ALU.max, ALU.min)\
                    .then_inc(s_q_ve, 1)
            ve.wait_ge(s_q_ve, 8)
            ve.tensor_tensor(q_rest, q_rest, q_parts[1], ALU.subtract).then_inc(s_q_ve, 1)
            ve.wait_ge(s_q_ve, 11)
            ve.tensor_copy(q_parts[2], q_rest).then_inc(s_q_ve, 1)

        def group(g, last):
            wait(ve, s_xd, g * NC)
            wait(ve, s_t, g * (NC - 1))
            for k, a in enumerate((dt_t, dtw_t, ecum_t, etot_t)):
                ve.tensor_scalar(head_g[:, k, :, :], a[:, :, bass.ds(g * HG, HG)], 1.0, None, ALU.mult)\
                    .then_inc(s_head, 1)
            ve.tensor_scalar(d_g[:], d_b[:, bass.ds(g * HG, HG)], 1.0, None, ALU.mult).then_inc(s_head, 1)
            for c in range(NC):
                n = g * NC + c
                st = g * (NC - 1) + c
                first = isinstance(g, int) and n == 0
                left, made = conv_tiles(g, last, c)
                made = made[:1]
                if not first:
                    variance(n - 1, (c - 1) % 2)
                ve.wait_ge(s_gb, n + 1)
                wait(ve, s_gm, 2 * n)
                wait(ve, s_m, 2 * n)
                ve.tensor_tensor(gm[:], p_gb[:, 0:P], tri[:], ALU.mult).then_inc(s_gm, 1)
                ve.tensor_copy(b_tok[:], p_gb[:, P:2 * P]).then_inc(s_gm, 1)
                if not first:
                    z_rest(n - 1)
                ve.wait_ge(s_gm, 2 * (n + 1))
                for k in range(2):
                    ve.wait_ge(s_e, 2 * n + k + 1)
                    m = em[:, c % 2, k * 512:(k + 1) * 512].rearrange("p (h t) -> p h t", h=HG // 2)
                    ve.tensor_tensor(m, m, gm[:].unsqueeze(1).broadcast_to([P, HG // 2, P]), ALU.mult)\
                        .then_inc(s_m, 1)
                if not last:
                    for w in SPLIT_IN.get(c, ()):
                        if w in VE_LO:
                            w_rest(g + 1, w)
                for tile in left:
                    first_tap(*tile)
                    second_tap(*tile)
                    last_tap(*tile)
                if not left:
                    for tile in made:
                        first_tap(*tile)
                if not first:
                    residual(n - 1, (c - 1) % NC)
                for tile in left:
                    silu(*tile)
                if not left:
                    for tile in made:
                        second_tap(*tile)
                        last_tap(*tile)
                if c > 0:
                    ve.wait_ge(s_inter, st)
                    ve.wait_ge(s_head, 5 * (g + 1))
                    wait(ve, s_ss, n - 1)
                    wait(ve, s_z, n - 1)
                    ve.tensor_tensor(by_head(y[:, c % 2, :]), by_head(p_in[:]), heads(ECUM, c), ALU.mult)\
                        .then_inc(s_t, 1)
                ve.wait_ge(s_stn, n + 1)
                wait(ve, s_stu, n)
                if c > 0:
                    ve.wait_ge(s_std, st)
                    ve.tensor_tensor(state[:], p_x[:], state_dec[:], ALU.add).then_inc(s_stu, 1)
                else:
                    ve.tensor_copy(state[:], p_x[:]).then_inc(s_stu, 1)
                for tile in made:
                    if left:
                        first_tap(*tile)
                        second_tap(*tile)
                    else:
                        silu(*tile)
                if c == 0:
                    w_rest(g, TILES + KT)
                    w_rest(g, TILES + KT + 1)
                ve.wait_ge(s_intra, n + 1)
                if c > 0:
                    ve.wait_ge(s_txd, st)
                    ve.tensor_tensor(y[:, c % 2, :], y[:, c % 2, :], p_y[:], ALU.add).then_inc(s_y, 1)
                else:
                    ve.wait_ge(s_xd, n + 1)
                    wait(ve, s_ss, n - 1)
                    wait(ve, s_z, n - 1)
                    ve.tensor_tensor(y[:, c % 2, :], x_d[:], p_y[:], ALU.add).then_inc(s_y, 1)
                ve.wait_ge(s_y, n + 1)
                ve.wait_ge(s_sg, n + 1)
                wait(ve, s_zt, n)
                ve.tensor_tensor(z[:], y[:, c % 2, :], gate[:], ALU.mult).then_inc(s_z, 1)
                if left:
                    for tile in made:
                        last_tap(*tile)
                        silu(*tile)
                if last:
                    for k in {4: (0, 1), 5: (2, 3), 6: (4, 5), 7: (6,)}.get(c, ()):
                        row_stats(g, k)
                    if c == NC - 2:
                        small_operands()
                if not (last and c == NC - 1):
                    gate_silu(n + 1)
                if c == 0:
                    w_rest(g, TILES + KT + 2)
                    w_rest(g, TILES + KT + 3)

        def ln_rest(c):
            ve.wait_ge(ln_hi, c + 1)
            ve.tensor_tensor(xn_lo[:, :, c * P:(c + 1) * P], (p_x, p_in)[c % 2][:].rearrange("p (k t) -> p k t", k=KT),
                             xn_hi[:, :, c * P:(c + 1) * P].bitcast(F32), ALU.subtract).then_inc(ln_lo, 1)

        for c in range(NC + 3):
            if c < NC:
                ve.wait_ge(s_x[c], 16)
                ve.bn_stats(stats[:, c, :], x_res[:, c, :]).then_inc(ln_st, 1)
            if 2 <= c < NC + 2:
                ve.wait_ge(ln_rs, c)
                wait(ve, ln_tr, c - 3)
                ve.tensor_scalar(xnt[:, c % 2, :], x_res[:, c - 2, :], mean_var[:, c - 2, 0:1],
                                 rstd[:, c - 2:c - 1], ALU.subtract, ALU.mult).then_inc(ln_xn, 1)
            if c < NC:
                ve.wait_ge(ln_st, c + 1)
                ve.bn_aggr(mean_var[:, c, :], stats[:, c, :]).then_inc(ln_var, 1)
            if 3 <= c:
                ln_rest(c - 3)
            if c < NC:
                ve.wait_ge(ln_var, 2 * c + 1)
                ve.tensor_scalar(rstd[:, c:c + 1], mean_var[:, c, 1:2], EPS, None, ALU.add).then_inc(ln_var, 1)
            if c == CH:
                ve.wait_ge(s_const, 16 * 7)
                ve.tensor_scalar(conv_w[:], conv_w[:], 0.5, None, ALU.mult).then_inc(s_halved, 1)
                ve.tensor_scalar(norm_w[:], norm_w[:], 0.5, None, ALU.mult).then_inc(s_halved, 1)
            if c == CH + 1:
                ve.tensor_copy(w_hi[:, WT - 1, :], z[:]).then_inc(dt_ve, 1)
                ve.memset(t_mask, 1.0).then_inc(dt_ve, 1)
                ve.wait_ge(dt_ve, 2)
                ve.tensor_tensor(w_lo[:, WT - 1, :], z[:], w_hi[:, WT - 1, :].bitcast(F32), ALU.subtract)\
                    .then_inc(s_split_dt, 1)
                ve.memset(t_mask[:, 0:HALF:P], 0.0).then_inc(s_split_dt, 1)
        for a in range(2):
            rows = slice(a * H, (a + 1) * H)
            ve.wait_ge(dt_mm, a + 1)
            ve.tensor_scalar(t_v[rows], (p_d0, p_d1)[a][rows, :], head_c[rows, 0:1], None, ALU.add)\
                .then_inc(dt_ve, 1)
        ve.wait_ge(dt_ac, 2)
        ve.tensor_scalar(t_w, t_e, 1.0, None, ALU.add).then_inc(dt_ve, 1)
        ve.wait_ge(dt_ve, 5)
        ve.tensor_scalar(t_dt, t_w, -1.0, None, ALU.add).then_inc(dt_ve, 1)
        ve.reciprocal(t_rem, t_w).then_inc(dt_ve, 1)
        ve.wait_ge(dt_ve, 7)
        ve.tensor_tensor(t_dt, t_e, t_dt, ALU.subtract).then_inc(dt_ve, 1)
        ve.wait_ge(dt_ve, 8)
        ve.tensor_tensor(t_dt, t_dt, t_rem, ALU.mult).then_inc(dt_ve, 1)
        ve.wait_ge(dt_ve, 9)
        ve.wait_ge(dt_ac, 4)
        ve.tensor_tensor(t_dt, t_dt, t_r, ALU.add).then_inc(dt_ve, 1)
        ve.tensor_scalar(t_v, t_v, 0.0, None, ALU.max).then_inc(dt_ve, 1)
        ve.wait_ge(dt_ve, 11)
        ve.tensor_tensor(t_dt, t_dt, t_v, ALU.add).then_inc(ln_st, 1)
        ve.tensor_scalar(head_c[:, 2:3], head_c[:, 3:4], -1.0, None, ALU.mult).then_inc(ln_st, 1)
        ve.wait_ge(ln_st, NC + 2)
        ve.tensor_scalar(t_a, t_dt, head_c[:, 2:3], LOG_FLOOR, ALU.mult, ALU.max).then_inc(ln_st, 1)
        ve.wait_ge(ln_st, NC + 3)
        ve.wait_ge(s_split_dt, 2)
        ve.tensor_tensor_scan(t_cum, t_mask, t_a, 0.0, ALU.mult, ALU.add).then_inc(ln_st, 1)
        ve.wait_ge(ln_st, NC + 4)
        cum_c = t_cum.rearrange("p (c t) -> p c t", t=P)
        ve.tensor_tensor(t_rem.rearrange("p (c t) -> p c t", t=P), cum_c[:, :, P - 1:P].broadcast_to([P, CH, P]),
                         cum_c, ALU.subtract).then_inc(dt_ve, 1)
        ve.tensor_copy(t_parts[0], t_cum).then_inc(dt_ve, 1)
        ve.wait_ge(dt_ve, 13)
        ve.tensor_tensor(t_r, t_cum, t_parts[0], ALU.subtract).then_inc(ln_st, 1)
        ve.wait_ge(ln_st, NC + 5)
        ve.tensor_copy(t_parts[1], t_r).then_inc(dt_ve, 1)
        ve.wait_ge(dt_ve, 14)
        ve.tensor_tensor(t_parts[2], t_r, t_parts[1], ALU.subtract).then_inc(dt_ve, 1)
        first_tap(0, 0, 0, 0)
        second_tap(0, 0, 0, 0)
        last_tap(0, 0, 0, 0)
        ve.wait_ge(dt_tp, 4)
        ve.tensor_copy(by_half(dt_t), transposed(p_gate)).then_inc(dt_ve, 1)
        w_rest(0, TILES)
        w_rest(0, TILES + 1)
        for j in range(TILES):
            if j + 1 < TILES:
                first_tap(j + 1, 0, j + 1, 0)
                second_tap(j + 1, 0, j + 1, 0)
            silu(j, 0, j, 0)
            if j + 1 < TILES:
                last_tap(j + 1, 0, j + 1, 0)
        ve.wait_ge(dt_ac, 7)
        ve.wait_ge(dt_ve, 16)
        ve.tensor_tensor(dtw_t[:], dtw_t[:], dt_t[:], ALU.mult).then_inc(dt_ve, 1)
        ve.wait_ge(dt_ve, 17)
        gate_silu(0)
        group(0, False)
        with ve.Fori(1, G - 1) as g:
            group(g, False)
        group(G - 1, True)
        variance_of(slice(0, NC - 1))
        variance(LAST, (NC - 1) % 2)
        z_rest(LAST)
        residual(LAST, NC - 1)
        row_stats(G - 1, NC - 1)
        variance_of(slice(NC - 1, NC))

    @block.tensor
    def _(pe):
        def conv_tile(T, g, j, hf, bank=None):
            wait(pe, s_cin, 2 * T if bank is None else 2 * (T - 1))
            if hf == 0:
                pe.wait_ge(s_whi, g * WT + j + 1)
                pe.wait_ge(*lo_count(g, j))
            three_pass(pe, (p_d1 if bank else p_tile)[:],
                       lambda k: (w_hi[:, j, k * P:(k + 1) * P], w_lo[:, j, k * P:(k + 1) * P]),
                       lambda k: (xn_hi[:, k, half_cols(hf)], xn_lo[:, k, half_cols(hf)]), KT).then_inc(s_prj, 1)

        def z_transpose(m):
            pe.wait_ge(s_z, m + 1)
            for k in range(GW // P):
                mm = pe.transpose(p_in[:, k * P:(k + 1) * P], z[:, k * P:(k + 1) * P], ident[:])
            mm.then_inc(s_zt, 1)

        def gate_product(m, c):
            wait(pe, s_sg, m)
            cs = slice(c * P, (c + 1) * P)
            three_pass(pe, p_gate[:], lambda k: (xn_hi[:, k, cs], xn_lo[:, k, cs]),
                       lambda k: (w_hi[:, TILES + k, :], w_lo[:, TILES + k, :]), KT).then_inc(s_gate, 1)

        def next_gate(g, last, n, c):
            if c + 1 < NC:
                gate_product(n + 1, c + 1)
            elif not last:
                pe.wait_ge(s_whi, (g + 1) * WT + TILES + KT)
                pe.wait_ge(*lo_count(g + 1, TILES + 1))
                pe.wait_ge(*lo_count(g + 1, TILES + KT - 1))
                gate_product(n + 1, 0)

        def out_product(m):
            pe.wait_ge(s_zlo, m + 1)
            three_pass(pe, p_y[:], lambda k: (zt_hi[:, k, :], zt_lo[:, k, :]),
                       lambda k: (w_hi[:, TILES + KT + k, :], w_lo[:, TILES + KT + k, :]), GW // P).then_inc(s_out, 1)

        def group(g, last):
            for c in range(NC):
                n = g * NC + c
                first = isinstance(g, int) and n == 0
                left, made = conv_tiles(g, last, c)
                cs = slice(c * P, (c + 1) * P)
                if c % CH == 0:
                    pe.wait_ge(s_xc, (2 * g + c // CH + 1) * TILES)
                wait(pe, s_stu, n)
                for j in range(GW // P):
                    mm = pe.transpose(p_x[:, j * P:(j + 1) * P], xbc[:, j, cs], ident[:])
                mm.then_inc(s_xt, 1)
                if not first:
                    z_transpose(n - 1)
                wait(pe, s_gm, 2 * n)
                pe.transpose(p_gb[:, P:2 * P], xbc[:, TB, cs], ident[:])
                pe.matmul(p_gb[:, 0:P], xbc[:, TB, cs], xbc[:, TC, cs], start=True, stop=True).then_inc(s_gb, 1)
                pe.wait_ge(s_dl[c % 2], 32 * (g * (NC // 2) + c // 2 + 1))
                wait(pe, s_e, 2 * n)
                for k, p in enumerate((p_d0, p_d1)):
                    mm = pe.matmul(p[:], d_lhs[:, c % 2, :], d_rhs[:, c % 2, k * 512:(k + 1) * 512],
                                   start=True, stop=True)
                mm.then_inc(s_d, 1)
                for tile in made[:1]:
                    conv_tile(*tile)
                if not made:
                    next_gate(g, last, n, c)
                if c == 1:
                    pe.wait_ge(s_whi, (g + 1) * WT)
                    pe.wait_ge(*lo_count(g, WT - 1))
                if not first:
                    out_product(n - 1)
                if c > 0:
                    pe.wait_ge(s_stu, n)
                    pe.wait_ge(s_zlo, n)
                    pe.matmul(p_in[:], xbc[:, TC, cs], state[:], start=True, stop=True).then_inc(s_inter, 1)
                pe.wait_ge(s_gm, 2 * (n + 1))
                pe.wait_ge(s_xw, n + 1)
                pe.wait_ge(s_xs, n + 1)
                pe.matmul(p_x[:], b_tok[:], x_w[:], start=True, stop=True).then_inc(s_stn, 1)
                pe.wait_ge(s_m, 2 * (n + 1))
                pe.wait_ge(s_xdt, n + 1)
                wait(pe, s_res, n)
                for h in range(HG):
                    mm = pe.matmul(p_y[:, h * HD:(h + 1) * HD], em[:, c % 2, h * P:(h + 1) * P],
                                   x_dt[:, h * HD:(h + 1) * HD], start=True, stop=True)
                mm.then_inc(s_intra, 1)
                if made:
                    next_gate(g, last, n, c)
                for tile in made[1:]:
                    conv_tile(*tile)

        pe.wait_ge(s_const, 16 * 7)
        for c in range(NC):
            pe.wait_ge(ln_xn, c + 1)
            wait(pe, ln_lo, c - 1)
            for k in range(KT):
                mm = pe.transpose((p_x, p_in)[c % 2][:, k * P:(k + 1) * P], xnt[:, c % 2, k * P:(k + 1) * P], ident[:])
            mm.then_inc(ln_tr, 1)
        pe.wait_ge(s_split_dt, 1)
        for a in range(2):
            pe.wait_ge(ln_lo, CH * (a + 1))
            three_pass(pe, (p_d0, p_d1)[a][:],
                       lambda k: (w_hi[:, WT - 1, k * P:(k + 1) * P], w_lo[:, WT - 1, k * P:(k + 1) * P]),
                       lambda k: (xn_hi[:, k, half_cols(a)], xn_lo[:, k, half_cols(a)]), KT).then_inc(dt_mm, 1)
        conv_tile(0, 0, 0, 0)
        pe.wait_ge(dt_ve, 4)
        conv_tile(1, 0, 1, 0, 1)
        pe.wait_ge(dt_ve, 12)
        for src, dst in ((t_dt, p_gate), (t_cum, p_y), (t_rem, p_gb), (None, p_d0)):
            for b in range(CH):
                rows_c = src[:, b * P:(b + 1) * P] if src is not None \
                    else t_cum[:, (b + 1) * P - 1:(b + 1) * P].broadcast_to([P, P])
                mm = pe.transpose(dst[:, b * P:(b + 1) * P], rows_c, ident[:])
            mm.then_inc(dt_tp, 1)
        for j in range(2, TILES):
            conv_tile(j, 0, j, 0, j % 2)
        pe.wait_ge(dt_ve, 16)
        pe.wait_ge(s_whi, TILES + KT)
        pe.wait_ge(*lo_count(0, TILES + 1))
        pe.wait_ge(*lo_count(0, TILES + KT - 1))
        gate_product(0, 0)
        group(0, False)
        with pe.Fori(1, G - 1) as g:
            group(g, False)
        group(G - 1, True)
        z_transpose(LAST)
        out_product(LAST)


def swiglu_up(nc, io, ctx, x_res, h, wd_hi, wd_lo, ident, mean_var, rstd, q_prep):
    def sb(name, shape, dt=F32):
        return ctx.enter_context(nc.sbuf_tensor(name, shape, dt))

    def pb(name):
        return ctx.enter_context(nc.psum_tensor(name, [P, 512], F32))

    def sem(name):
        return ctx.enter_context(nc.semaphore(name))

    xn_hi = sb("f_xn_hi", [P, KT, L], F32R)
    xn_lo = sb("f_xn_lo", [P, KT, L], F32R)
    q = sb("q_words", [P, 3, 512], I32)
    q4 = sb("q4", [P, 2, 512], I32)
    wz = sb("wz", [P, 2, 512])
    wf = sb("wf", [P, 2, 512])
    w_hi = sb("f_w_hi", [P, 2, 512], F32R)
    w_lo = sb("f_w_lo", [P, 2, 512], F32R)
    g_th = sb("g_th", [P, 2, HALF])
    g_act = sb("g_act", [P, 2, HALF])
    rows = sb("f_rows", [P, 2, D])
    shift = sb("q_shift", [P, 1], I32)
    sc_gu = sb("sc_gu_parts", [PART * GU, 2 * NI], BF16)
    sc_d = sb("sc_d_parts", [P, D], BF16)
    zp_gu = sb("zp_gu", [GU, 8, 2 * NI // 8], BF16)
    zp_d = sb("zp_d", [P, 8, D // 8], BF16)
    hot_gu = sb("hot_gu", [PART * GU, 2 * D], BF16)
    hot_d = sb("hot_d", [P, NI], BF16)
    row_of = sb("row_groups", [PART * GD, 2])
    gi_gu = wz[0:PART * GU, :, :].rearrange("p a n -> p (a n)")
    gi_d0 = g_act[0:PART * GD, :, :].rearrange("p a n -> p (a n)")
    gi_d1 = g_th[0:PART * GD, 0, 0:NI - L]

    p_z, p_s, p_g, p_u = ([pb(f"p_{k}{i}") for i in range(2)] for k in "zsgu")
    p_n = p_g + p_u
    f_zero = sem("f_zero")
    f_small, f_gi, f_scales, f_hot = (sem(f"f_{k}") for k in ("small", "gi", "scales", "hot"))
    ln_xn, ln_tr, ln_hi, ln_lo = (sem(f"fln_{k}") for k in "abcd")
    s_q = [sem(f"f_q{m}") for m in range(3)]
    s_dq, s_g, s_u = (sem(f"f_pe_{k}") for k in ("dq", "g", "u"))
    s_unp, s_wz, s_wf, s_ga, s_h = (sem(f"f_ve_{k}") for k in ("unp", "wz", "wf", "ga", "h"))
    s_hi, s_th, s_lo, s_lod = sem("f_act_hi"), sem("f_act_th"), sem("f_pool_lo"), sem("f_ve_lod")

    q_rows = io["q"].rearrange("u p n -> (u p) n")
    block = ctx.enter_context(nc.Block())
    LAST_T = NT - 1

    def is_last(t):
        return isinstance(t, int) and t == LAST_T

    def dest(wd, w, t, m):
        return wd[:, bass.ds(t, 1), :].rearrange("p a n -> p (a n)") if m == 2 else w[:, m, :]

    def both_tiles(eng, tile):
        tile(0, 0)
        tile(1, 1)
        with eng.Fori(1, NT // 2) as i:
            tile(2 * i, 0)
            tile(2 * i + 1, 1)
        tile(LAST_T, LAST_T % 2)

    def half_of(hf):
        return slice(hf * HALF, (hf + 1) * HALF)

    @block.sync
    def _(sp):
        def load_q(t, m):
            row = at(sp, (3 * t + m) * P)
            wait(sp, s_unp, 3 * t + m - 2)
            sp.dma_start(q[:, m, :], q_rows[bass.ds(row, P), :]).then_inc(s_q[m], 16)

        sp.dma_start(shift[:], io["shift"]).then_inc(f_small, 16)
        sp.dma_start(row_of[:], io["row_of"]).then_inc(f_small, 16)
        index = {k: q_prep[k].rearrange("p n -> (p n)").unsqueeze(0) for k in ("gi_gu", "gi_d")}
        sp.dma_start(gi_gu, index["gi_gu"].broadcast_to([PART * GU, 2 * D])).then_inc(f_gi, 16)
        sp.dma_start(gi_d0, index["gi_d"][:, 0:L].broadcast_to([PART * GD, L])).then_inc(f_gi, 16)
        sp.dma_start(gi_d1, index["gi_d"][:, L:NI].broadcast_to([PART * GD, NI - L])).then_inc(f_gi, 16)
        sp.dma_start(sc_gu[:], q_prep["sc_gu"].rearrange("k p n -> (k p n)").rearrange("(r n) -> r n", n=2 * NI))\
            .then_inc(f_scales, 16)
        sp.dma_start(zp_gu[:], q_prep["zp_gu"].rearrange("p n -> (p n)").rearrange("(i g n) -> g i n", i=8, g=GU))\
            .then_inc(f_scales, 16)
        for m in range(2):
            load_q(0, m)
        sp.wait_ge(f_zero, 3)
        sp.dma_start(sc_d[0:PART * GD, :], q_prep["sc_d"].rearrange("k p n -> (k p n)")
                     .rearrange("(r n) -> r n", n=D)).then_inc(f_scales, 16)
        sp.dma_start(zp_d[0:GD, :, :], q_prep["zp_d"].rearrange("p n -> (p n)").rearrange("(i g n) -> g i n", i=8, g=GD))\
            .then_inc(f_scales, 16)
        load_q(0, 2)
        for m in range(3):
            load_q(1, m)
        with sp.Fori(2, NT) as t:
            for m in range(3):
                load_q(t, m)

    @block.gpsimd
    def _(pool):
        def rest(t, m, slot):
            pool.wait_ge(s_hi, 3 * t + m + 1)
            pool.tensor_tensor(w_lo[:, m, :], wf[:, slot, :], w_hi[:, m, :].bitcast(F32), ALU.subtract)\
                .then_inc(s_lo, 1)

        for a in (sc_d, zp_d, hot_d):
            pool.memset(a[:], 0.0).then_inc(f_zero, 1)
        rest(0, 0, 0)
        rest(0, 1, 1)

        def tile(t, odd):
            if not is_last(t):
                rest(t + 1, 0, 1 - odd)
                rest(t + 1, 1, odd)

        both_tiles(pool, tile)

    @block.scalar
    def _(act):
        def round_w(t, m, slot):
            u = 3 * t + m
            act.wait_ge(s_wf, u + 1)
            if m < 2:
                wait(act, (s_g, s_u)[m], 2 * t)
            act.activation(dest(wd_hi, w_hi, t, m), wf[:, slot, :], ACT.Copy).then_inc(s_hi, 1)

        def tanh(t, hf):
            act.wait_ge(s_g, 2 * t + hf + 1)
            wait(act, s_ga, 2 * t + hf - 1)
            act.activation(g_th[:, hf, :], p_g[hf][:], ACT.Tanh, scale=0.5).then_inc(s_th, 1)

        for c in range(NC):
            act.wait_ge(ln_tr, c + 1)
            act.activation(xn_hi[:, :, c * P:(c + 1) * P], p_n[c % 4][:].rearrange("p (k t) -> p k t", k=KT),
                           ACT.Copy).then_inc(ln_hi, 1)
        round_w(0, 0, 0)
        round_w(0, 1, 1)

        def tile(t, odd):
            round_w(t, 2, odd)
            tanh(t, 0)
            tanh(t, 1)
            if not is_last(t):
                round_w(t + 1, 0, 1 - odd)
                round_w(t + 1, 1, odd)

        both_tiles(act, tile)

    @block.vector
    def _(ve):
        def dequant(t, m, slot):
            u = 3 * t + m
            ve.wait_ge(s_q[m], 16 * (t + 1))
            wait(ve, s_wz, u - 1)
            ve.tensor_scalar(q4[:, slot, :], q[:, m, :], shift[:, 0:1], 15, ALU.logical_shift_right,
                             ALU.bitwise_and).then_inc(s_unp, 1)
            ve.wait_ge(s_dq, u + 1)
            ve.wait_ge(s_unp, u + 1)
            wait(ve, s_wf, u - 1)
            ve.tensor_tensor(wz[:, slot, :], q4[:, slot, :], p_z[slot][:], ALU.subtract).then_inc(s_wz, 1)
            ve.wait_ge(s_wz, u + 1)
            if m == 1:
                wait(ve, s_lod, t)
            else:
                wait(ve, s_lo, 2 * t + m // 2)
            ve.tensor_tensor(wf[:, slot, :], wz[:, slot, :], p_s[slot][:], ALU.mult).then_inc(s_wf, 1)

        def norm_rows(c):
            wait(ve, ln_tr, c - 1)
            ve.tensor_scalar(rows[:, c % 2, :], x_res[:, c, :], mean_var[:, c, 0:1], rstd[:, c:c + 1],
                             ALU.subtract, ALU.mult).then_inc(ln_xn, 1)

        def norm_rest(c):
            ve.wait_ge(ln_hi, c + 1)
            ve.tensor_tensor(xn_lo[:, :, c * P:(c + 1) * P], p_n[c % 4][:].rearrange("p (k t) -> p k t", k=KT),
                             xn_hi[:, :, c * P:(c + 1) * P].bitcast(F32), ALU.subtract).then_inc(ln_lo, 1)

        def one_hot(index, hot, col):
            ve.tensor_scalar(hot, index, row_of[0:hot.shape[0], col:col + 1], None, ALU.is_equal).then_inc(f_hot, 1)

        for c in range(NC + 2):
            if c < NC:
                norm_rows(c)
            if c >= 2:
                norm_rest(c - 2)
            if c == CH + 1:
                ve.wait_ge(f_small, 32)
                ve.wait_ge(f_gi, 48)
                ve.wait_ge(f_zero, 3)
                one_hot(gi_gu, hot_gu[:], 0)
                one_hot(gi_d0, hot_d[0:PART * GD, 0:L], 1)
                one_hot(gi_d1, hot_d[0:PART * GD, L:NI], 1)
        ve.wait_ge(f_hot, 3)
        dequant(0, 0, 0)
        dequant(0, 1, 1)

        def gate(t, hf):
            ve.wait_ge(s_th, 2 * t + hf + 1)
            wait(ve, s_h, 2 * t + hf - 1)
            ve.scalar_tensor_tensor(out=g_act[:, hf, :], in0=g_th[:, hf, :], scalar=1.0, in1=p_g[hf][:],
                                    op0=ALU.add, op1=ALU.mult).then_inc(s_ga, 1)

        def down_rest(t, slot):
            ve.wait_ge(s_hi, 3 * t + 3)
            ve.tensor_tensor(wd_lo[:, bass.ds(t, 1), :].rearrange("p a n -> p (a n)"), wf[:, slot, :],
                             dest(wd_hi, w_hi, t, 2).bitcast(F32), ALU.subtract).then_inc(s_lod, 1)

        def inner(t, hf):
            ve.wait_ge(s_u, 2 * t + hf + 1)
            ve.wait_ge(s_ga, 2 * t + hf + 1)
            ve.scalar_tensor_tensor(out=h[:, bass.ds(t, 1), half_of(hf)].rearrange("p a t -> p (a t)"),
                                    in0=g_act[:, hf, :], scalar=0.5, in1=p_u[hf][:],
                                    op0=ALU.mult, op1=ALU.mult).then_inc(s_h, 1)

        def tile(t, odd):
            dequant(t, 2, odd)
            gate(t, 0)
            gate(t, 1)
            down_rest(t, odd)
            if not is_last(t):
                dequant(t + 1, 0, 1 - odd)
            inner(t, 0)
            if not is_last(t):
                dequant(t + 1, 1, odd)
            inner(t, 1)

        both_tiles(ve, tile)

    @block.tensor
    def _(pe):
        def spread(t, m, slot):
            u = 3 * t + m
            wait(pe, s_wf, u - 1)
            if m == 2:
                rows_t = bass.ds(t * P, P)
                pe.matmul(p_z[slot][:], hot_d[:, rows_t], zp_d[:].rearrange("g i n -> g n i"), start=True, stop=True)
                pe.matmul(p_s[slot][:], hot_d[:, rows_t], sc_d[:], start=True, stop=True).then_inc(s_dq, 1)
                return
            cols = bass.ds(m * NI + t * P, P)
            words = zp_gu[:, :, bass.ds(m * (NI // 8) + t * (P // 8), P // 8)].rearrange("g i n -> g n i")
            for k in range(KT):
                r = slice(m * D + k * P, m * D + (k + 1) * P)
                pe.matmul(p_z[slot][:, k * P:(k + 1) * P], hot_gu[0:GU, r], words, start=True, stop=True)
            for k in range(KT):
                r = slice(m * D + k * P, m * D + (k + 1) * P)
                mm = pe.matmul(p_s[slot][:, k * P:(k + 1) * P], hot_gu[:, r], sc_gu[:, cols], start=True, stop=True)
            mm.then_inc(s_dq, 1)

        def product(t, m, hf):
            p, done = ((p_g, s_g), (p_u, s_u))[m]
            wait(pe, (s_ga, s_h)[m], 2 * t + hf - 1)
            if hf == 0:
                pe.wait_ge(s_lo, 2 * t + m + 1)
            three_pass(pe, p[hf][:],
                       lambda k: (w_hi[:, m, k * P:(k + 1) * P], w_lo[:, m, k * P:(k + 1) * P]),
                       lambda k: (xn_hi[:, k, half_of(hf)], xn_lo[:, k, half_of(hf)]), KT).then_inc(done, 1)

        for c in range(NC):
            pe.wait_ge(ln_xn, c + 1)
            wait(pe, ln_lo, c - 3)
            for k in range(KT):
                mm = pe.transpose(p_n[c % 4][:, k * P:(k + 1) * P], rows[:, c % 2, k * P:(k + 1) * P], ident[:])
            mm.then_inc(ln_tr, 1)
        pe.wait_ge(f_hot, 3)
        pe.wait_ge(f_scales, 64)
        spread(0, 0, 0)
        spread(0, 1, 1)
        spread(0, 2, 0)
        pe.wait_ge(ln_lo, NC)

        def tile(t, odd):
            product(t, 0, 0)
            product(t, 0, 1)
            if not is_last(t):
                spread(t + 1, 0, 1 - odd)
            product(t, 1, 0)
            if not is_last(t):
                spread(t + 1, 1, odd)
            product(t, 1, 1)
            if not is_last(t):
                spread(t + 1, 2, 1 - odd)

        both_tiles(pe, tile)


DH = 16
HQ = 32
HK = 8
REP = HQ // HK
QW = DH * HK
KVW = DH * HK
QKV = QW + 2 * KVW
D_VE = 11

E = 8
RANK = 16
ER = E * RANK
LORA_SCALE = 2.0


def token_tiles(nc, io, ctx, x_res, h, wd_hi, wd_lo, ident):
    def sb(name, shape, dt=F32):
        return ctx.enter_context(nc.sbuf_tensor(name, shape, dt))

    def pb(name):
        return ctx.enter_context(nc.psum_tensor(name, [P, 512], F32))

    def sem(name):
        return ctx.enter_context(nc.semaphore(name))

    h_hi, h_lo = sb("h_hi", [P, 2, NT, P], F32R), sb("h_lo", [P, 2, NT, P], F32R)
    n2_hi, n2_lo = sb("n2_hi", [P, KT, P], F32R), sb("n2_lo", [P, KT, P], F32R)
    n3_hi, n3_lo = sb("n3_hi", [P, KT, P], F32R), sb("n3_lo", [P, KT, P], F32R)
    hw_hi, hw_lo = sb("hw_hi", [P, P], F32R), sb("hw_lo", [P, P], F32R)
    qkv_hi, qkv_lo = sb("qkv_hi", [P, KT, QKV], F32R), sb("qkv_lo", [P, KT, QKV], F32R)
    wb_hi, wb_lo = sb("wb_hi", [P, KT, D], F32R), sb("wb_lo", [P, KT, D], F32R)
    wa_hi, wa_lo = sb("wa_hi", [P, KT, ER + E], F32R), sb("wa_lo", [P, KT, ER + E], F32R)
    wl_hi, wl_lo = sb("wl_hi", [P, D], F32R), sb("wl_lo", [P, D], F32R)
    prod = sb("prod", [P, DH * DH * HK])
    wq_sum = sb("wq_sum", [P, KT, QW])
    n2_raw = wq_sum
    wkv_raw = sb("wkv_raw", [P, KT, 2 * KVW])
    wa_raw = sb("wa_raw", [P, KT, ER + E])
    wl_raw = sb("wl_raw", [P, D])
    b_qkv = sb("b_qkv", [P, QKV])
    b_base = sb("b_base_rows", [P, D])
    rows2, rows3 = sb("rows2", [P, D]), sb("rows3", [P, D])
    qkv = sb("qkv", [P, QKV])
    s = sb("scores", [P, DH, DH])
    mx = sb("score_max", [P, DH])
    den = sb("score_sum", [P, DH])
    o = sb("att_out", [P, DH, HK])
    st2, st3 = sb("t_st2", [P, 6]), sb("t_st3", [P, 6])
    mv2, mv3 = sb("t_mv2", [P, 2]), sb("t_mv3", [P, 2])
    rs2, rs3 = sb("t_rs2", [P, 2]), sb("t_rs3", [P, 2])
    m_half = sb("t_m_half", [P, 1])
    lg, m8, w8, w8b, expert = (sb(f"route_{k}", [P, E]) for k in ("lg", "m8", "w8", "w8b", "iota"))
    i8 = sb("route_i8", [P, E], U32)
    sel = sb("route_sel", [P, 2])
    rt = sb("route_rt", [P, 3])
    hw = sb("hw", [P, ER])
    out_t = sb("out_t", [P, D])
    bq_raw = out_t

    p_a, p_t2, p_t3, p_t4, p_b, p_c, p_r = (pb(f"t_p_{k}") for k in ("a", "t2", "t3", "t4", "b", "c", "r"))

    w_in = [sem(f"t_in{k}") for k in range(4)]
    w_wb, w_sum, w_hi_s, w_lo_s, w_lo_b, c_pool = (
        sem(f"t_{k}") for k in ("wb", "sum", "whi", "wlo", "wlob", "cpool"))
    s_a, s_t2, s_t3, s_t4, s_b, s_r, s_c, s_dl = (
        sem(f"t_pe_{k}") for k in ("a", "t2", "t3", "t4", "b", "r", "c", "dl"))
    a_h, a_n2, a_n3, a_hw, a_exp, a_rt = (sem(f"t_act_{k}") for k in ("h", "n2", "n3", "hw", "exp", "rt"))
    g_h, g_lo2, g_m1, g_m2, g_rs2, g_rs3, g_xb = (
        sem(f"t_pool_{k}") for k in ("h", "lo2", "m1", "m2", "rs2", "rs3", "xb"))
    v_add, v_ln2, v_n2, v_qkv, v_m1, v_s, v_den, v_att, v_x3, v_ln3, v_n3, v_lo3, v_rt, v_hw, v_lo4, v_fin = (
        sem(f"t_ve_{k}") for k in ("add", "ln2", "n2", "qkv", "m1", "s", "den", "att", "x3", "ln3",
                                   "n3", "lo3", "rt", "hw", "lo4", "fin"))
    s_store = sem("t_store")

    def flat(ap):
        return ap.rearrange("p a b -> p (a b)")

    def x_tile(c):
        return x_res[:, bass.ds(c, 1), :].rearrange("p a n -> p (a n)")

    def score_product(eng, d0, d1):
        n = d1 - d0
        q = qkv[:, d0 * HK:d1 * HK].rearrange("p (d h) -> p d h", h=HK).unsqueeze(2).broadcast_to([P, n, DH, HK])
        k = qkv[:, QW:QW + KVW].rearrange("p (e h) -> p e h", h=HK).unsqueeze(1).broadcast_to([P, n, DH, HK])
        o4 = prod[:, d0 * DH * HK:d1 * DH * HK].rearrange("p (d e h) -> p d e h", e=DH, h=HK)
        return eng.tensor_tensor(o4, q, k, ALU.mult)

    def value_product(eng, d0, d1):
        n = d1 - d0
        a = s[:, d0:d1, :].unsqueeze(2).broadcast_to([P, n, HK, DH])
        v = qkv[:, QW + KVW:QKV].rearrange("p (e h) -> p h e", h=HK).unsqueeze(1).broadcast_to([P, n, HK, DH])
        o4 = prod[:, d0 * DH * HK:d1 * DH * HK].rearrange("p (d h e) -> p d h e", h=HK, e=DH)
        return eng.tensor_tensor(o4, a, v, ALU.mult)

    def weights():
        return ((qkv_hi[:, :, 0:QW], qkv_lo[:, :, 0:QW], wq_sum[:]),
                (qkv_hi[:, :, QW:], qkv_lo[:, :, QW:], wkv_raw[:]),
                (wa_hi[:], wa_lo[:], wa_raw[:]),
                (wl_hi[:], wl_lo[:], wl_raw[:]),
                (flat(wb_hi[:]), flat(wb_lo[:]), prod[:]))

    def pipeline(step, first=0):
        for i in range(first, NC + 3):
            step(i)

    def live(c):
        return not isinstance(c, int) or 0 <= c < NC

    block = ctx.enter_context(nc.Block())

    @block.sync
    def _(sp):
        sp.dma_start(prod[:], io["wq"]).then_inc(w_in[0], 16)
        sp.dma_start(flat(wkv_raw[:]), io["wkv"]).then_inc(w_in[1], 16)
        sp.dma_start(bq_raw[:], io["bq"].broadcast_to([P, DH * HQ])).then_inc(w_in[2], 16)
        sp.dma_start(b_qkv[:, QW:], io["bkv"].broadcast_to([P, 2 * KVW])).then_inc(w_in[2], 16)
        sp.dma_start(expert[:], io["expert"].broadcast_to([P, E])).then_inc(w_in[2], 16)
        sp.dma_start(b_base[:], io["b_base"].broadcast_to([P, D])).then_inc(w_in[2], 16)
        sp.dma_start(flat(wa_raw[:]), io["wa"]).then_inc(w_in[3], 16)
        sp.dma_start(wl_raw[:], io["wl"]).then_inc(w_in[3], 16)
        sp.wait_ge(w_sum, 1)
        sp.dma_start(prod[:], io["wb"]).then_inc(w_wb, 16)

        def step(i):
            if live(i - 3):
                sp.wait_ge(v_fin, i - 2)
                sp.dma_start(io["out"][bass.ds((i - 3) * P, P), :], out_t[:]).then_inc(s_store, 16)

        pipeline(step)
        sp.wait_ge(s_store, 16 * NC)

    @block.gpsimd
    def _(pool):
        pool.memset(m_half[:], -0.5).then_inc(c_pool, 1)

        def h_rest(c):
            pool.wait_ge(a_h, c + 1)
            pool.tensor_tensor(h_lo[:, c % 2, :, :], h[:, :, c * P:(c + 1) * P], h_hi[:, c % 2, :, :].bitcast(F32), ALU.subtract)\
                .then_inc(g_h, 1)

        h_rest(0)
        h_rest(1)
        for n, (hi, lo, raw) in enumerate(weights()[:-1]):
            pool.wait_ge(w_hi_s, n + 1)
            pool.tensor_tensor(lo, raw, hi.bitcast(F32), ALU.subtract).then_inc(w_lo_s, 1)

        def step(i):
            b, c = i - 1, i - 2
            if live(c):
                pool.wait_ge(a_exp, c + 1)
                pool.wait_ge(v_den, 4 * c + 3)
                value_product(pool, D_VE, DH).then_inc(g_m2, 1)
            if live(b):
                pool.wait_ge(a_n2, 2 * (b + 1))
                pool.tensor_tensor(flat(n2_lo[:]), flat(n2_raw[:]), flat(n2_hi[:]).bitcast(F32), ALU.subtract)\
                    .then_inc(g_lo2, 1)
            if 0 < i < NC - 1:
                h_rest(i + 1)
            if live(c):
                pool.wait_ge(v_ln3, 3 * (c + 1))
                pool.tensor_tensor(rs3[:, 1:2], rs3[:, 0:1], m_half[:], ALU.pow).then_inc(g_rs3, 1)
                pool.wait_ge(v_n3, c + 1)
                pool.tensor_tensor(x_tile(c), x_tile(c), b_base[:], ALU.add).then_inc(g_xb, 1)
            if i < NC:
                pool.wait_ge(v_ln2, 3 * (i + 1))
                pool.tensor_tensor(rs2[:, 1:2], rs2[:, 0:1], m_half[:], ALU.pow).then_inc(g_rs2, 1)
            if live(b):
                pool.wait_ge(v_qkv, b + 1)
                wait(pool, v_att, 3 * b)
                score_product(pool, D_VE, DH).then_inc(g_m1, 1)

        pool.wait_ge(c_pool, 1)
        pool.wait_ge(w_in[2], 64)
        pipeline(step)

    @block.scalar
    def _(act):
        def h_round(c):
            wait(act, s_a, c - 1)
            act.activation(h_hi[:, c % 2, :, :], h[:, :, c * P:(c + 1) * P], ACT.Copy).then_inc(a_h, 1)

        h_round(0)
        h_round(1)
        for n, (hi, lo, raw) in enumerate(weights()):
            if n == 0:
                act.wait_ge(w_sum, 1)
            if n == 1:
                act.wait_ge(w_in[1], 16)
            if n == 2:
                act.wait_ge(w_in[3], 32)
            if n == 4:
                act.wait_ge(w_wb, 16)
            act.activation(hi, raw, ACT.Copy).then_inc(w_hi_s, 1)

        def step(i):
            b, c, d = i - 1, i - 2, i - 3
            if 0 < i < NC - 1:
                h_round(i + 1)
            if live(b):
                act.wait_ge(s_t2, b + 1)
                wait(act, s_b, b)
                wait(act, g_lo2, b)
                if b == 0:
                    act.wait_ge(w_lo_s, 1)
                act.activation(flat(n2_raw[:]), p_t2[:], ACT.Copy).then_inc(a_n2, 1)
                act.activation(flat(n2_hi[:]), p_t2[:], ACT.Copy).then_inc(a_n2, 1)
            if live(d):
                act.wait_ge(s_t4, d + 1)
                wait(act, s_dl, d)
                act.activation(hw_hi[:], p_t4[:, 0:P], ACT.Copy).then_inc(a_hw, 1)
            if live(c):
                act.wait_ge(s_t3, c + 1)
                wait(act, s_c, c)
                act.activation(flat(n3_hi[:]), p_t3[:], ACT.Copy).then_inc(a_n3, 1)
            if live(c):
                act.wait_ge(v_rt, 8 * c + 2)
                act.activation(rt[:, 0:1], m8[:, 0:1], ACT.Exp, scale=-1.0, bias=m8[:, 1:2]).then_inc(a_rt, 1)
            if live(b):
                act.wait_ge(v_den, 4 * b + 3)
                act.activation(flat(s[:]), flat(s[:]), ACT.Exp, scale=1.0 / float(np.sqrt(DH))).then_inc(a_exp, 1)

        pipeline(step)

    @block.vector
    def _(ve):
        ve.wait_ge(w_in[0], 16)
        ve.tensor_reduce(flat(wq_sum[:]), prod[:].rearrange("p (n r) -> p n r", r=REP), AX.X, ALU.add).then_inc(w_sum, 1)
        ve.wait_ge(w_in[2], 64)
        ve.tensor_reduce(b_qkv[:, 0:QW], bq_raw[:].rearrange("p (n r) -> p n r", r=REP), AX.X, ALU.add)\
            .then_inc(w_sum, 1)

        def layer_stats(x, st, mv, rs, count, c):
            ve.bn_stats(st[:], x).then_inc(count, 1)
            ve.wait_ge(count, 3 * c + 1)
            ve.bn_aggr(mv[:], st[:]).then_inc(count, 1)
            ve.wait_ge(count, 3 * c + 2)
            ve.tensor_scalar(rs[:, 0:1], mv[:, 1:2], EPS, None, ALU.add).then_inc(count, 1)

        def step(i):
            b, c, d = i - 1, i - 2, i - 3
            k = 8 * c
            if live(c):
                ve.wait_ge(a_exp, c + 1)
                ve.tensor_reduce(den[:], s[:], AX.X, ALU.add).then_inc(v_den, 1)
                value_product(ve, 0, D_VE).then_inc(v_att, 1)
                ve.wait_ge(v_den, 4 * (c + 1))
                ve.reciprocal(den[:], den[:]).then_inc(v_att, 1)
                ve.wait_ge(v_att, 3 * c + 2)
                ve.wait_ge(g_m2, c + 1)
                ve.tensor_reduce(flat(o[:]), prod[:].rearrange("p (n e) -> p n e", e=DH), AX.X, ALU.add)\
                    .then_inc(v_att, 1)
            if live(d):
                ve.wait_ge(a_hw, d + 1)
                ve.tensor_tensor(hw_lo[:], p_t4[:, 0:P], hw_hi[:].bitcast(F32), ALU.subtract).then_inc(v_lo4, 1)
            if live(c):
                ve.wait_ge(v_att, 3 * (c + 1))
                ve.tensor_tensor(o[:], o[:], den[:].unsqueeze(2).broadcast_to([P, DH, HK]), ALU.mult).then_inc(v_x3, 1)
                ve.wait_ge(v_x3, 2 * c + 1)
                x = x_tile(c).rearrange("p (n r) -> p n r", r=REP)
                ve.tensor_tensor(x, x, flat(o[:]).unsqueeze(2).broadcast_to([P, QW, REP]), ALU.add).then_inc(v_x3, 1)
                ve.wait_ge(v_x3, 2 * (c + 1))
                layer_stats(x_tile(c), st3, mv3, rs3, v_ln3, c)
                ve.wait_ge(g_rs3, c + 1)
                wait(ve, s_t3, c)
                ve.tensor_scalar(rows3[:], x_tile(c), mv3[:, 0:1], rs3[:, 1:2], ALU.subtract, ALU.mult).then_inc(v_n3, 1)
            if live(i):
                ve.wait_ge(s_a, i + 1)
                ve.tensor_tensor(x_tile(i), x_tile(i), p_a[:], ALU.add).then_inc(v_add, 1)
            if live(i):
                ve.wait_ge(v_add, i + 1)
                layer_stats(x_tile(i), st2, mv2, rs2, v_ln2, i)
            if live(c):
                ve.wait_ge(a_n3, c + 1)
                ve.tensor_tensor(flat(n3_lo[:]), p_t3[:], flat(n3_hi[:]).bitcast(F32), ALU.subtract).then_inc(v_lo3, 1)
            if live(d):
                ve.wait_ge(s_dl, d + 1)
                ve.wait_ge(g_xb, d + 1)
                wait(ve, s_store, 16 * d)
                ve.tensor_tensor(out_t[:], x_tile(d), p_c[:], ALU.add).then_inc(v_fin, 1)
            if live(i):
                ve.wait_ge(g_rs2, i + 1)
                wait(ve, s_t2, i)
                ve.tensor_scalar(rows2[:], x_tile(i), mv2[:, 0:1], rs2[:, 1:2], ALU.subtract, ALU.mult).then_inc(v_n2, 1)
            if live(b):
                ve.wait_ge(s_b, b + 1)
                wait(ve, v_att, 3 * b)
                ve.tensor_tensor(qkv[:], p_b[:, 0:QKV], b_qkv[:], ALU.add).then_inc(v_qkv, 1)
                ve.wait_ge(v_qkv, b + 1)
                score_product(ve, 0, D_VE).then_inc(v_m1, 1)
            if live(c):
                ve.wait_ge(s_r, c + 1)
                ve.tensor_copy(lg[:], p_r[:, ER:ER + E]).then_inc(v_rt, 1)
                ve.wait_ge(v_rt, k + 1)
                ve.max(m8[:], lg[:]).then_inc(v_rt, 1)
                ve.wait_ge(v_rt, k + 2)
                ve.max_index(i8[:], m8[:], lg[:]).then_inc(v_rt, 1)
                ve.wait_ge(v_rt, k + 3)
                ve.tensor_copy(sel[:], i8[:, 0:2]).then_inc(v_rt, 1)
            if live(b):
                ve.wait_ge(v_m1, b + 1)
                ve.wait_ge(g_m1, b + 1)
                ve.tensor_reduce(flat(s[:]), prod[:].rearrange("p (n h) -> p n h", h=HK), AX.X, ALU.add).then_inc(v_den, 1)
                ve.wait_ge(v_den, 4 * b + 1)
                ve.tensor_reduce(mx[:], s[:], AX.X, ALU.max).then_inc(v_den, 1)
                ve.wait_ge(v_den, 4 * b + 2)
                ve.tensor_tensor(s[:], s[:], mx[:].unsqueeze(2).broadcast_to([P, DH, DH]), ALU.subtract)\
                    .then_inc(v_den, 1)
            if live(c):
                ve.wait_ge(a_rt, c + 1)
                ve.tensor_scalar(rt[:, 1:2], rt[:, 0:1], 1.0, None, ALU.add).then_inc(v_rt, 1)
                ve.wait_ge(v_rt, k + 5)
                ve.reciprocal(rt[:, 2:3], rt[:, 1:2]).then_inc(v_rt, 1)
                ve.tensor_scalar(w8b[:], expert[:], sel[:, 1:2], rt[:, 0:1], ALU.is_equal, ALU.mult).then_inc(v_rt, 1)
                ve.wait_ge(v_rt, k + 7)
                ve.scalar_tensor_tensor(out=w8[:], in0=expert[:], scalar=sel[:, 0:1], in1=w8b[:],
                                        op0=ALU.is_equal, op1=ALU.add).then_inc(v_rt, 1)
                ve.wait_ge(v_rt, k + 8)
                ve.tensor_scalar(w8b[:], w8[:], rt[:, 2:3], LORA_SCALE, ALU.mult, ALU.mult).then_inc(v_hw, 1)
                ve.wait_ge(v_hw, 2 * c + 1)
                ve.tensor_tensor(hw[:].rearrange("p (e r) -> p e r", e=E), p_r[:, 0:ER].rearrange("p (e r) -> p e r", e=E),
                                 w8b[:].unsqueeze(2).broadcast_to([P, E, RANK]), ALU.mult).then_inc(v_hw, 1)

        step(0)
        hi, lo, raw = weights()[-1]
        ve.wait_ge(w_hi_s, len(weights()))
        ve.tensor_tensor(lo, raw, hi.bitcast(F32), ALU.subtract).then_inc(w_lo_b, 1)
        ve.wait_ge(w_lo_b, 1)
        pipeline(step, 1)

    @block.tensor
    def _(pe):
        def down(i, k0, k1):
            hi, lo = h_hi[:, i % 2, :, :], h_lo[:, i % 2, :, :]
            for k in range(k0, k1):
                for n, (x, w) in enumerate(((hi, wd_hi), (hi, wd_lo), (lo, wd_hi))):
                    mm = pe.matmul(p_a[:], x[:, k, :], w[:, k, :], start=(k == 0 and n == 0),
                                   stop=(k == NT - 1 and n == 2))
            return mm

        NT_FIRST = 3

        def down_start(i):
            if live(i):
                pe.wait_ge(g_h, i + 1)
                wait(pe, v_add, i)
                down(i, 0, NT_FIRST)

        def step(i):
            b, c, d = i - 1, i - 2, i - 3
            if live(i):
                down(i, NT_FIRST, NT_FIRST + (NT - NT_FIRST) // 2)
            if live(b):
                pe.wait_ge(v_n2, b + 1)
                wait(pe, a_n2, 2 * b)
                for k in range(KT):
                    mm = pe.transpose(p_t2[:, k * P:(k + 1) * P], rows2[:, k * P:(k + 1) * P], ident[:])
                mm.then_inc(s_t2, 1)
            if live(i):
                down(i, NT_FIRST + (NT - NT_FIRST) // 2, NT).then_inc(s_a, 1)
            if live(d):
                pe.wait_ge(v_hw, 2 * (d + 1))
                wait(pe, v_lo4, d)
                pe.transpose(p_t4[:, 0:P], hw[:], ident[:]).then_inc(s_t4, 1)
            if live(b):
                pe.wait_ge(g_lo2, b + 1)
                wait(pe, v_qkv, b)
                if b == 0:
                    pe.wait_ge(w_lo_s, 2)
                three_pass(pe, p_b[:, 0:QKV], lambda k: (n2_hi[:, k, :], n2_lo[:, k, :]),
                           lambda k: (qkv_hi[:, k, :], qkv_lo[:, k, :]), KT).then_inc(s_b, 1)
            if live(d):
                pe.wait_ge(v_lo4, d + 1)
                for n, (x, w) in enumerate(((hw_hi, wl_hi), (hw_hi, wl_lo), (hw_lo, wl_hi))):
                    mm = pe.matmul(p_c[:], x[:], w[:], start=False, stop=(n == 2))
                mm.then_inc(s_dl, 1)
            if live(c):
                pe.wait_ge(v_n3, c + 1)
                wait(pe, v_lo3, c)
                for k in range(KT):
                    mm = pe.transpose(p_t3[:, k * P:(k + 1) * P], rows3[:, k * P:(k + 1) * P], ident[:])
                mm.then_inc(s_t3, 1)
            down_start(i + 1)
            if live(c):
                pe.wait_ge(v_lo3, c + 1)
                wait(pe, v_hw, 2 * c)
                if c == 0:
                    pe.wait_ge(w_lo_s, 4)
                    pe.wait_ge(w_lo_b, 1)
                three_pass(pe, p_r[:, 0:ER + E], lambda k: (n3_hi[:, k, :], n3_lo[:, k, :]),
                           lambda k: (wa_hi[:, k, :], wa_lo[:, k, :]), KT).then_inc(s_r, 1)
                wait(pe, v_fin, c)
                for k in range(KT):
                    for n, (x, w) in enumerate(((n3_hi, wb_hi), (n3_hi, wb_lo), (n3_lo, wb_hi))):
                        mm = pe.matmul(p_c[:], x[:, k, :], w[:, k, :], start=(k == 0 and n == 0), stop=False)
                mm.then_inc(s_c, 1)

        down_start(0)
        pipeline(step)


def program(nc, io, stages=4):
    with ExitStack() as outer:
        def sb(ctx, name, shape, dt=F32):
            return ctx.enter_context(nc.sbuf_tensor(name, shape, dt))
        x_res = sb(outer, "x_res", [P, NC, D])
        ident = sb(outer, "identity", [P, P])
        mean_var = sb(outer, "mean_var2", [P, NC, 2])
        rstd = sb(outer, "rstd2", [P, NC])
        q_prep = {k: nc.dram_tensor(f"q_{k}", shape, dt, kind="Internal").ap() for k, shape, dt in (
            ("sc_gu", [PART, P, NSC], BF16), ("sc_d", [PART, P, NSD], BF16), ("zp_gu", [P, NSC], BF16),
            ("zp_d", [P, NSD], BF16), ("gi_gu", [P, NGI], F32), ("gi_d", [P, NGD], F32))}
        with ExitStack() as ctx:
            mixer(nc, io, ctx, x_res, ident, mean_var, rstd, q_prep)
        with ExitStack() as held:
            h = sb(held, "h", [P, NT, L])
            wd_hi = sb(held, "wd_hi", [P, NT, D], F32R)
            wd_lo = sb(held, "wd_lo", [P, NT, D], F32R)
            with ExitStack() as ctx:
                swiglu_up(nc, io, ctx, x_res, h, wd_hi, wd_lo, ident, mean_var, rstd, q_prep)
            with ExitStack() as ctx:
                token_tiles(nc, io, ctx, x_res, h, wd_hi, wd_lo, ident)


def layouts(v):
    f = {k: np.ascontiguousarray(np.asarray(a)) for k, a in v.items()}
    io = {"x": f["L0_attn_hidden_states"].reshape(L, D)}
    wi = f["L0_attn_in_proj_w"]
    inner = H * HD
    gate, x, b, c, dt = np.split(wi, np.cumsum([inner, inner, G * NS, G * NS]), axis=0)

    def conv_rows(a):
        a, ab, ac = a
        return np.concatenate([a.reshape((G, GW // P, P) + a.shape[1:]), ab.reshape((G, 1, P) + a.shape[1:]),
                               ac.reshape((G, 1, P) + a.shape[1:])], axis=1)
    cw = conv_rows((x, b, c)).reshape(G, TILES, P, KT, P).transpose(0, 1, 4, 3, 2).reshape(G, TILES, P, 512)
    gw = gate.reshape(G, GW, KT, P).transpose(0, 2, 3, 1)
    ow = f["L0_attn_out_proj_w"].reshape(D, G, GW // P, P).transpose(1, 2, 3, 0)
    io["w"] = np.concatenate([cw, gw, ow], axis=1).reshape(G * WT, P, 512)
    dt2 = np.concatenate([dt, dt], axis=0)
    io["w_dt"] = dt2.reshape(P, KT, P).transpose(2, 1, 0).reshape(P, 512)
    kw = np.concatenate([f["L0_attn_conv_weight"], f["L0_attn_conv_bias"][:, None]], axis=1)
    io["conv_w"] = conv_rows(np.split(kw, [inner, inner + G * NS])).transpose(2, 0, 1, 3)
    io["norm_w"] = f["L0_attn_norm_weight"].reshape(G, GW // P, P).transpose(2, 0, 1)
    hc = np.stack([f["L0_attn_dt_bias"], f["L0_attn_A_log"]], axis=1)
    io["head_c"] = np.concatenate([hc, hc], axis=0)
    io["d"] = f["L0_attn_D"].reshape(1, H)
    io["ident"] = np.eye(P, dtype=np.float32)
    io["tri"] = np.triu(np.ones((P, P), np.float32))
    t = np.arange(P)
    thr = 2 * np.arange(1, NTHR + 1)
    lhs = np.zeros((KD, P), np.float32)
    lhs[:PART] = 1
    lhs[PART + PART * HG:] = t[None] >= thr[:, None]
    rhs = np.zeros((KD, HG, P), np.float32)
    for k in range(PART):
        for h in range(HG):
            rhs[PART + k * HG + h, h] = -1
    rhs[PART + PART * HG:] = MASK * (t[None] < thr[:, None])[:, None, :]
    io["d_lhs"] = lhs.astype(np.dtype("bfloat16"))
    io["d_rhs"] = rhs.reshape(KD, HG * P).astype(np.dtype("bfloat16"))

    def pad(a, n, axis):
        w = [(0, 0)] * a.ndim
        w[axis] = (0, n - a.shape[axis])
        return np.pad(a, w)
    gu = [np.repeat(pad(f[f"L0_ffn_{m}_qweight"], NI, 1), 8, axis=0).reshape(KT, P, NT, P).transpose(2, 1, 0, 3)
          .reshape(NT, P, 512) for m in ("gate", "up")]
    dn = np.repeat(pad(f["L0_ffn_down_qweight"], NI // 8, 0), 8, axis=0).reshape(NT, P, D)
    io["q"] = np.stack([gu[0], gu[1], dn], axis=1).reshape(3 * NT, P, 512)
    scales = [np.concatenate([pad(f[f"L0_ffn_{m}_scales"], NI, 1) for m in ("gate", "up")], axis=1),
              f["L0_ffn_down_scales"]]
    zeros = [np.concatenate([pad(f[f"L0_ffn_{m}_qzeros"], NI // 8, 1) for m in ("gate", "up")], axis=1),
             f["L0_ffn_down_qzeros"]]
    index = [np.concatenate([f["L0_ffn_gate_g_idx"], f["L0_ffn_up_g_idx"]]), pad(f["L0_ffn_down_g_idx"], NI, 0)]
    io["q_scales"] = np.concatenate([a.reshape(P, -1) for a in scales], axis=1)
    io["q_zeros"] = np.tile(np.concatenate([a.reshape(P // 8, -1) for a in zeros], axis=1), (8, 1))
    io["q_index"] = np.concatenate([a.reshape(P, -1) for a in index], axis=1)
    io["z_shift"] = (4 * (np.arange(P) // (P // 8))).astype(np.int32).reshape(P, 1)
    io["shift"] = (4 * (np.arange(P) % 8)).astype(np.int32).reshape(P, 1)
    n = np.arange(PART * GD)
    io["row_of"] = np.stack([n % GU, n % GD], axis=1).astype(np.float32)

    def by_row(a):
        return a.reshape(KT, P, -1).transpose(1, 0, 2).reshape(P, -1)
    io["wq"] = by_row(f["L1_attn_Wq"])
    io["wkv"] = by_row(np.concatenate([f["L1_attn_Wk"].reshape(D, -1), f["L1_attn_Wv"].reshape(D, -1)], axis=1))
    io["bq"] = f["L1_attn_bq"].reshape(1, -1)
    io["bkv"] = np.concatenate([f["L1_attn_bk"].reshape(-1), f["L1_attn_bv"].reshape(-1)]).reshape(1, -1)
    io["wb"] = by_row(f["L1_ffn_W_base"].T)
    io["b_base"] = f["L1_ffn_b_base"].reshape(1, -1)
    io["wa"] = by_row(np.concatenate([f["L1_ffn_A"].reshape(ER, D), f["L1_ffn_W_router"]], axis=0).T)
    io["wl"] = f["L1_ffn_B"].transpose(0, 2, 1).reshape(ER, D)
    io["expert"] = np.arange(E, dtype=np.float32).reshape(1, E)
    return {k: np.ascontiguousarray(a) for k, a in io.items()}


def kernel(**inputs):
    import concourse.bacc as bacc
    from concourse.bass_utils import run_bass_kernel_spmd

    arrays = layouts(inputs)
    nc = bacc.Bacc("TRN2", target_bir_lowering=False, num_devices=1)
    io = {k: nc.dram_tensor(k, a.shape, mybir.dt.from_np(a.dtype), kind="ExternalInput").ap()
          for k, a in arrays.items()}
    io["out"] = nc.dram_tensor("out", (L, D), F32, kind="ExternalOutput").ap()
    program(nc, io)
    r = run_bass_kernel_spmd(nc, [arrays], core_ids=[0])
    return r.results[0]["out"].reshape(1, L, D)
```
